# Optimizing a Trainium2 kernel written in Bass

```python
import numpy as np
import jax
import jax.numpy as jnp

def _softmax(x, axis=-1):
    return jax.nn.softmax(x, axis=axis)

def _gelu(x):
    return jax.nn.gelu(x, approximate=True)

def _silu(x):
    return jax.nn.silu(x)

def _sigmoid(x):
    return jax.nn.sigmoid(x)

def _layernorm(x, axis=-1, eps=1e-05):
    m = jnp.mean(x, axis=axis, keepdims=True)
    v = jnp.var(x, axis=axis, keepdims=True)
    return (x - m) / jnp.sqrt(v + eps)

def _scatter_add(tgt, idx, src, axis=0):
    return tgt.at[idx].add(src)

def _segment_sum(src, seg, n):
    return jax.ops.segment_sum(src, seg, n)
kernel_name = 'mk_macaron_d1_jaxref_r8_b2c473'

def setup_inputs(seed: int=0):
    np.random.seed(seed)
    _w = jnp.asarray

    def _L0_attn_setup():
        import jax, jax.numpy as jnp
        import numpy as np
        HIDDEN = 512
        HEAD_DIM = 128
        N_Q_HEADS = 32
        N_KV_HEADS = 8
        SLIDING_WINDOW = 128
        ROPE_THETA = 10000.0
        BATCH, SEQ = (1, 256)

        def _rope(t, pos):
            d = t.shape[-1]
            half = d // 2
            inv_freq = ROPE_THETA ** (-jnp.arange(half, dtype=jnp.float32) / half)
            ang = pos[:, None].astype(jnp.float32) * inv_freq[None, :]
            cos = jnp.cos(ang)[None, :, None, :]
            sin = jnp.sin(ang)[None, :, None, :]
            t1, t2 = (t[..., :half], t[..., half:])
            return jnp.concatenate([t1 * cos - t2 * sin, t1 * sin + t2 * cos], axis=-1)
        key = jax.random.key(seed)
        ks = jax.random.split(key, 5)
        w_scale = HIDDEN ** (-0.5)
        return {'x': jax.random.normal(ks[0], (BATCH, SEQ, HIDDEN), jnp.float32), 'wq': jax.random.normal(ks[1], (HIDDEN, N_Q_HEADS * HEAD_DIM), jnp.float32) * w_scale, 'wk': jax.random.normal(ks[2], (HIDDEN, N_KV_HEADS * HEAD_DIM), jnp.float32) * w_scale, 'wv': jax.random.normal(ks[3], (HIDDEN, N_KV_HEADS * HEAD_DIM), jnp.float32) * w_scale, 'wo': jax.random.normal(ks[4], (N_Q_HEADS * HEAD_DIM, HIDDEN), jnp.float32) * w_scale}
    _L0_attn_in = _L0_attn_setup()

    def _L0_ffn_setup():
        import jax, jax.numpy as jnp
        import numpy as np
        B, S, D, O, E, R = (2, 512, 512, 512, 8, 16)
        TOP_K = 2
        SCALING = 32.0 / 16.0
        key = jax.random.key(seed)
        k = jax.random.split(key, 6)
        x = jax.random.normal(k[0], (B, S, D), dtype=jnp.float32)
        W_base = jax.random.normal(k[1], (O, D), dtype=jnp.float32) * 0.02
        b_base = jax.random.normal(k[2], (O,), dtype=jnp.float32) * 0.02
        W_router = jax.random.normal(k[3], (E, D), dtype=jnp.float32) * 0.01
        lora_A = jax.random.normal(k[4], (E, R, D), dtype=jnp.float32) * (1.0 / np.sqrt(D))
        lora_B = jax.random.normal(k[5], (E, O, R), dtype=jnp.float32) * 0.02
        return {'x': x, 'W_base': W_base, 'b_base': b_base, 'W_router': W_router, 'lora_A': lora_A, 'lora_B': lora_B}
    _L0_ffn_in = _L0_ffn_setup()
    _d = {'L0_attn_x': _L0_attn_in['x'], 'L0_attn_wq': _L0_attn_in['wq'], 'L0_attn_wk': _L0_attn_in['wk'], 'L0_attn_wv': _L0_attn_in['wv'], 'L0_attn_wo': _L0_attn_in['wo'], 'L0_ffn_W_base': _L0_ffn_in['W_base'], 'L0_ffn_b_base': _L0_ffn_in['b_base'], 'L0_ffn_W_router': _L0_ffn_in['W_router'], 'L0_ffn_lora_A': _L0_ffn_in['lora_A'], 'L0_ffn_lora_B': _L0_ffn_in['lora_B']}
    _x0 = _d['L0_attn_x']
    _d['L0_attn_x'] = jax.random.normal(jax.random.fold_in(jax.random.key(seed), 1), (4, 256, 512), dtype=_x0.dtype)
    del _x0
    return _d

def reference(L0_attn_x, L0_attn_wq, L0_attn_wk, L0_attn_wv, L0_attn_wo, L0_ffn_W_base, L0_ffn_b_base, L0_ffn_W_router, L0_ffn_lora_A, L0_ffn_lora_B):

    def _L0_attn_ref(x, wq, wk, wv, wo):
        import jax, jax.numpy as jnp
        import numpy as np
        HIDDEN = 512
        HEAD_DIM = 128
        N_Q_HEADS = 32
        N_KV_HEADS = 8
        SLIDING_WINDOW = 128
        ROPE_THETA = 10000.0
        BATCH, SEQ = (1, 256)

        def _rope(t, pos):
            d = t.shape[-1]
            half = d // 2
            inv_freq = ROPE_THETA ** (-jnp.arange(half, dtype=jnp.float32) / half)
            ang = pos[:, None].astype(jnp.float32) * inv_freq[None, :]
            cos = jnp.cos(ang)[None, :, None, :]
            sin = jnp.sin(ang)[None, :, None, :]
            t1, t2 = (t[..., :half], t[..., half:])
            return jnp.concatenate([t1 * cos - t2 * sin, t1 * sin + t2 * cos], axis=-1)
        B, S, _ = x.shape
        G = N_Q_HEADS // N_KV_HEADS
        sm_scale = HEAD_DIM ** (-0.5)
        q = (x @ wq).reshape(B, S, N_Q_HEADS, HEAD_DIM)
        k = (x @ wk).reshape(B, S, N_KV_HEADS, HEAD_DIM)
        v = (x @ wv).reshape(B, S, N_KV_HEADS, HEAD_DIM)
        pos = jnp.arange(S)
        q = _rope(q, pos)
        k = _rope(k, pos)
        qg = q.reshape(B, S, N_KV_HEADS, G, HEAD_DIM)
        scores = jnp.einsum('bqhgd,bshd->bhgqs', qg, k) * sm_scale
        i = pos[:, None]
        j = pos[None, :]
        allowed = (j <= i) & (j > i - SLIDING_WINDOW)
        neg = jnp.finfo(scores.dtype).min
        scores = jnp.where(allowed[None, None, None], scores, neg)
        attn = jax.nn.softmax(scores, axis=-1)
        out = jnp.einsum('bhgqs,bshd->bqhgd', attn, v).reshape(B, S, N_Q_HEADS * HEAD_DIM)
        return out @ wo

    def _L0_ffn_ref(x, W_base, b_base, W_router, lora_A, lora_B):
        import jax, jax.numpy as jnp
        import numpy as np
        B, S, D, O, E, R = (2, 512, 512, 512, 8, 16)
        TOP_K = 2
        SCALING = 32.0 / 16.0
        d = x.shape[-1]
        n_experts = W_router.shape[0]
        xf = x.reshape(-1, d)
        logits = xf @ W_router.T
        probs = jax.nn.softmax(logits, axis=-1)
        topk_p, topk_i = jax.lax.top_k(probs, TOP_K)
        topk_p = topk_p / jnp.sum(topk_p, axis=-1, keepdims=True)
        w = jnp.sum(jax.nn.one_hot(topk_i, n_experts, dtype=xf.dtype) * topk_p[..., None], axis=1)
        h = jnp.einsum('td,erd->ter', xf, lora_A)
        lora_out = jnp.einsum('ter,eor,te->to', h, lora_B, w) * SCALING
        base = x @ W_base.T + b_base
        return base + lora_out.reshape(x.shape[:-1] + (W_base.shape[0],))
    x = L0_attn_x
    x = x + 0.5 * _L0_ffn_ref(_layernorm(x, axis=-1), L0_ffn_W_base, L0_ffn_b_base, L0_ffn_W_router, L0_ffn_lora_A, L0_ffn_lora_B)
    x = x + _L0_attn_ref(_layernorm(x, axis=-1), L0_attn_wq, L0_attn_wk, L0_attn_wv, L0_attn_wo)
    x = x + 0.5 * _L0_ffn_ref(_layernorm(x, axis=-1), L0_ffn_W_base, L0_ffn_b_base, L0_ffn_W_router, L0_ffn_lora_A, L0_ffn_lora_B)
    return x

_drawn_inputs = setup_inputs


def setup_inputs(seed=0):
    import zlib

    import numpy as np

    out = dict(_drawn_inputs(seed))
    spreads = {}
    factors = {}
    for name, (base, spread) in spreads.items():
        noise = np.random.default_rng([zlib.crc32(name.encode()), seed]).standard_normal(out[name].shape)
        drawn = base * np.exp(spread * noise) if base else spread * noise
        out[name] = jnp.asarray(drawn.astype(out[name].dtype))
    for name, factor in factors.items():
        out[name] = (out[name] * factor).astype(out[name].dtype)
    return out
```

```python
from contextlib import ExitStack

import numpy as np
import concourse.bass as bass
import concourse.mybir as mybir
from concourse.alu_op_type import AluOpType as ALU

F32 = mybir.dt.float32
F32R = mybir.dt.float32r
I32 = mybir.dt.int32
ACT = mybir.ActivationFunctionType

P = 128
BATCH, SEQ, HID = 4, 256, 512
TOK = BATCH * SEQ
NT = TOK // P
KT = HID // P
HEADS, KV, DH = 32, 8, 128
G = HEADS // KV
WINDOW = 128
EXPERTS, RANK, OUT = 8, 16, 512
ER = EXPERTS * RANK
ARW = ER + EXPERTS
EPS = 1e-5
SCALE = DH ** -0.5
THETA = 10000.0
HALF = 512
HT = HALF // P
FAR = 3.0e38
FMAX = 3.4e38
RSQRT_MAGIC = 1597463007.0
NEWTON = 3
RING = 5
CHUNK = 9
SLOTS = 8
ENDS = {(12 * (m + 1) - 1) // CHUNK: m for m in range(6)}
PASSES = ((0, 0), (0, 1), (1, 0))

assert WINDOW == P and SEQ == 2 * P and OUT == HID and G * DH == HID


def constants():
    ident = np.eye(P, dtype=np.float32)
    i, j = np.arange(P)[:, None], np.arange(P)[None, :]
    causal, past = j <= i, j > i
    mask = np.where(np.concatenate([causal, past, causal], axis=1), 0.0, FAR).astype(np.float32)
    half = DH // 2
    inv = np.power(np.float32(THETA), -np.arange(half, dtype=np.float32) / np.float32(half)).astype(np.float32)
    ang = (inv[:, None] * np.arange(SEQ, dtype=np.float32)[None, :]).astype(np.float32)
    cos, sin = np.cos(ang).astype(np.float32), np.sin(ang).astype(np.float32)
    cos = np.concatenate([cos, cos], axis=0)
    sin = np.concatenate([-sin, sin], axis=0)
    neg = np.float32(-SCALE)
    rope = np.stack([cos, sin, neg * cos, neg * sin], axis=1).astype(np.float32)
    return ident, mask, np.ascontiguousarray(rope)


def macaron(nc, x_in, wq, wk, wv, wo, w_base, b_base, w_router, lora_a, lora_b, ident_in, mask_in, rope_in, out):
    ctx = ExitStack()
    with ctx:
        def sb(name, shape, dt=F32):
            return ctx.enter_context(nc.sbuf_tensor(name, shape, dt))

        def sem(name):
            return ctx.enter_context(nc.semaphore(name))

        x = sb("x", [P, NT, HID])
        xnT = [sb(f"xnT_{s}", [P, KT, TOK], F32R) for s in ("hi", "lo")]
        ident = sb("ident", [P, P])
        mask = sb("mask", [P, 3 * P])
        rope = sb("rope", [P, 4, SEQ])
        half_bias = sb("half_bias", [P, OUT])
        ar = [sb(f"ar_{s}", [P, KT, ARW], F32R) for s in ("hi", "lo")]
        lb = [sb(f"lb_{s}", [P, OUT], F32R) for s in ("hi", "lo")]
        raw = sb("raw", [P, RING, HID])
        wq_s = [sb(f"wq_{s}", [P, KT, G * DH], F32R) for s in ("hi", "lo")]
        wk_s = [sb(f"wk_{s}", [P, KT, DH], F32R) for s in ("hi", "lo")]
        wv_s = [sb(f"wv_{s}", [P, KT, DH], F32R) for s in ("hi", "lo")]
        wo_s = [sb(f"wo_{s}", [P, G, HID], F32R) for s in ("hi", "lo")]
        q = [sb(f"q_{s}", [P, 2, G, HALF], F32R) for s in ("hi", "lo")]
        k = [sb(f"k_{s}", [P, 2, HALF], F32R) for s in ("hi", "lo")]
        v = [sb(f"v_{s}", [P, 2, HT, DH], F32R) for s in ("hi", "lo")]
        swap = sb("swap", [P, 2, HID])
        rot = sb("rot", [P, 2, HID])
        sm = sb("sm", [P, 2, 3 * P])
        prob = sb("prob", [P, 2, 3 * P])
        pT = [sb(f"pT_{s}", [P, 3, G, P], F32R) for s in ("hi", "lo")]
        oT = [sb(f"oT_{s}", [P, 2, 2, G, P], F32R) for s in ("hi", "lo")]
        nmax = sb("nmax", [P, 2, 2])
        gate = sb("gate", [P, 1])
        rsum = sb("rsum", [P, 2, 2])
        rinv = sb("rinv", [P, 2, 2])
        stats = sb("stats", [P, NT, 6])
        mv = sb("mv", [P, NT, 2])
        var = sb("var", [P, NT])
        rstd = sb("rstd", [P, NT])
        nt1 = sb("nt1", [P, NT])
        nt2 = sb("nt2", [P, NT])
        top = sb("top", [P, 2, 8])
        esub = sb("esub", [P, 2, 8])
        ebuf = sb("ebuf", [P, 2, 2, 16])
        etop = sb("etop", [P, 2, 8])
        two = sb("two", [P, 2, 8])
        rest = sb("rest", [P, 2, 16])
        esum = sb("esum", [P, 2])
        einv = sb("einv", [P, 2])
        wgt = sb("wgt", [P, 2, 8])
        ones_b = prob[:, :, :].rearrange("p a c -> p (a c)")
        b_stage, ones = ones_b[0:1, 0:OUT], ones_b[0:1, OUT:OUT + P]
        wb = [q[s][:, 0, :, :] for s in range(2)]

        wb_keep = [nc.dram_tensor(f"wb_keep_{s}", [P, KT, OUT], F32, kind="Internal").ap() for s in ("hi", "lo")]

        bank = [ctx.enter_context(nc.psum_tensor(f"bank{i}", [P, 512], F32)) for i in range(8)]
        A, S, T, O, C = bank[0:2], bank[2:4], bank[4], bank[5:7], bank[7]
        OUTB = [[bank[4], bank[5]], [bank[6], bank[7]]]

        ident_landed, tables_landed = sem("ident_landed"), sem("tables_landed")
        x_landed = [sem(f"x_landed{i}") for i in range(NT // 2)]
        w_landed = [sem(f"ffn_w_landed{i}") for i in range(4)]
        la_landed, lbr_landed, b_landed = sem("lora_a_landed"), sem("lora_b_landed"), sem("bias_landed")
        preset = sem("preset")
        prep_tr, prep_hi, prep_lo = sem("prep_transposed"), sem("prep_hi"), sem("prep_lo")
        kept, refetched = sem("wb_kept"), sem("wb_refetched")
        step = sem("dve_step")
        xn_done, tr_done, xhi_done, xlo_done = sem("xn_done"), sem("xT_done"), sem("xT_hi"), sem("xT_lo")
        biased = sem("bias_added")
        ar_done, esub_done, e_done, hw_done = sem("ar_done"), sem("esub_done"), sem("e_done"), sem("hw_done")
        ht_done, hthi_done, htlo_done = sem("hT_done"), sem("hT_hi"), sem("hT_lo")
        out_done, x_out = sem("ffn_out_done"), sem("ffn_x_done")
        stored = sem("stored")
        raw_landed = [sem(f"raw_landed{i}") for i in range(RING)]
        conv_hi, conv_lo = sem("w_hi_done"), sem("w_lo_done")
        a_done, a_free = sem("proj_done"), sem("proj_bank_read")
        swap_done, t2_done, sum_done = sem("swap_done"), sem("sin_done"), sem("rope_sum_done")
        qhi_done, qlo_done, vhi_done = sem("qk_hi"), sem("qk_lo"), sem("v_hi")
        s_done, min_done, exp_done = sem("scores_done"), sem("min_done"), sem("exp_done")
        rinv_done, norm_done = sem("rinv_done"), sem("norm_done")
        t_done, pthi_done, ptlo_done = sem("pT_done"), sem("pT_hi"), sem("pT_lo")
        pv_done, othi_done, otlo_done = sem("pv_done"), sem("oT_hi"), sem("oT_lo")
        c_done, x_added = sem("wo_done"), sem("attn_x_done")

        def wait(eng, s, n):
            if not isinstance(n, int) or n > 0:
                eng.wait_ge(s, n)

        def wk_pos(g):
            return 10 * g

        def wq_pos(g, i):
            return 10 * g + 1 + i

        def wv_pos(g):
            return 10 * g + 5

        def wo_pos(g, i):
            return 10 * g + 6 + i

        block = ctx.enter_context(nc.Block())

        @block.sync
        def _(sp):
            sp.dma_start(ident[:, :], ident_in).then_inc(ident_landed, 16)
            xv = x_in.rearrange("b (s p) d -> p (b s) d", p=P)
            for i in range(NT // 2):
                sp.dma_start(x[:, 2 * i:2 * i + 2, :], xv[:, 2 * i:2 * i + 2, :]).then_inc(x_landed[i], 16)
            sp.dma_start(mask[:, :], mask_in).then_inc(tables_landed, 16)
            sp.dma_start(rope[:, :, :], rope_in).then_inc(tables_landed, 16)

            def piece(n, slot, count, src):
                wait(sp, conv_lo, n - RING + 1)
                sp.dma_start(raw[:, slot, :] if len(src.shape) == 2 else
                             raw[:, slot, :].rearrange("p (t n) -> p t n", t=KT), src).then_inc(raw_landed[slot], 16)

            def wk_src(w, g):
                return w[:, bass.ds(g * DH, DH)].rearrange("(t p) n -> p t n", p=P)

            def wq_src(g, i):
                return wq[i * P:(i + 1) * P, bass.ds(g * (G * DH), G * DH)]

            def group(g, last):
                order = [("o", i) for i in range(G)]
                if not last:
                    order += [("k", 0)] + [("q", i) for i in range(KT)] + [("v", 0)]
                for kind, i in order:
                    if kind == "k":
                        n, off, src = wk_pos(g + 1), 4, wk_src(wk, g + 1)
                    elif kind == "o":
                        n, off, src = wo_pos(g, i), i, wo[bass.ds(g * (G * DH) + i * DH, DH), :]
                    elif kind == "q":
                        n, off, src = wq_pos(g + 1, i), 5 + i, wq_src(g + 1, i)
                    else:
                        n, off, src = wv_pos(g + 1), 9, wk_src(wv, g + 1)
                    piece(n, (6 + off) % RING, None, src)

            sp.wait_ge(prep_tr, 5)
            piece(0, 0, None, wk_src(wk, 0))
            for i in range(KT):
                piece(1 + i, (1 + i) % RING, None, wq_src(0, i))
            piece(5, 5 % RING, None, wk_src(wv, 0))
            sp.wait_ge(prep_lo, 4)
            for s in range(2):
                sp.dma_start(wb_keep[s], wb[s].bitcast(F32)).then_inc(kept, 16)
            group(0, False)
            with sp.Fori(1, KV - 1) as g:
                group(g, False)
            group(KV - 1, True)
            sp.wait_ge(kept, 32)
            sp.wait_ge(s_done, SLOTS * (2 * KV - 1))
            for s in range(2):
                sp.dma_start(wb[s].bitcast(F32), wb_keep[s]).then_inc(refetched, 16)
            ov = out.rearrange("b (s p) d -> p (b s) d", p=P)
            for t in range(NT):
                sp.wait_ge(x_out, NT + t + 1)
                sp.dma_start(ov[:, t, :], x[:, t, :]).then_inc(stored, 16)
            sp.wait_ge(stored, 16 * NT)

        @block.gpsimd
        def _(pool):
            nc.gpsimd.memset(ones, 1.0).then_inc(preset, 1)
            nc.gpsimd.memset(ebuf[:, :, :, :], -1.0).then_inc(preset, 1)
            nc.gpsimd.memset(two[:, :, :], -1.0).then_inc(preset, 1)

            def bias(f):
                ln = 2 * f
                if f == 0:
                    pool.wait_ge(prep_hi, 8)
                for t in range(NT):
                    pool.wait_ge(xn_done, NT * ln + t + 1)
                    nc.gpsimd.tensor_tensor(x[:, t, :], x[:, t, :], half_bias[:, :], ALU.add).then_inc(biased, 1)

            def split_lo(n, slot, hi, lo):
                pool.wait_ge(conv_hi, n + 1)
                src = raw[:, slot, :]
                if len(hi.shape) == 3:
                    src = src.rearrange("p (t n) -> p t n", t=KT)
                nc.gpsimd.tensor_tensor(lo, src, hi.bitcast(F32), ALU.subtract).then_inc(conv_lo, 1)

            def rope_sin(j, m):
                r = 5 * j + m
                w = swap[:, m % 2, :].rearrange("p (b s) -> p b s", b=2)
                tab = rope[:, 1 if m == 0 else 3, :].unsqueeze(1).broadcast_to([P, 2, SEQ])
                pool.wait_ge(swap_done, r + 1)
                nc.gpsimd.tensor_tensor(w, w, tab, ALU.mult).then_inc(t2_done, 1)

            def rope_lo(j, m, par):
                r = 5 * j + m
                hi = k[0][:, par, :] if m == 0 else q[0][:, par, m - 1, :]
                lo = k[1][:, par, :] if m == 0 else q[1][:, par, m - 1, :]
                pool.wait_ge(qhi_done, r + 1)
                nc.gpsimd.tensor_tensor(lo, rot[:, m % 2, :], hi.bitcast(F32), ALU.subtract).then_inc(qlo_done, 1)

            def weights(g, hf, s, last):
                if hf == 0 and s in (4, 5):
                    for i in (2 * (s - 4), 2 * (s - 4) + 1):
                        split_lo(wo_pos(g, i), (6 + i) % RING, wo_s[0][:, i, :], wo_s[1][:, i, :])
                if hf == 0 and s == 6 and not last:
                    split_lo(wk_pos(g + 1), (6 + 4) % RING, wk_s[0][:, :, :], wk_s[1][:, :, :])
                if (hf, s) in ((0, 7), (1, 0)) and not last:
                    for i in ((0, 1) if hf == 0 else (2, 3)):
                        split_lo(wq_pos(g + 1, i), (6 + 5 + i) % RING, wq_s[0][:, i, :], wq_s[1][:, i, :])
                if hf == 1 and s == 2 and not last:
                    split_lo(wv_pos(g + 1), (6 + 9) % RING, wv_s[0][:, :, :], wv_s[1][:, :, :])

            def group(g, last):
                for hf in range(2):
                    for s in range(SLOTS):
                        m = ENDS.get(s, 5) if not (last and hf == 1) else 5
                        if m < 5:
                            rope_sin(2 * g + hf + 1, m)
                            rope_lo(2 * g + hf + 1, m, 1 - hf)
                        weights(g, hf, s, last)

            bias(0)
            split_lo(0, 0, wk_s[0][:, :, :], wk_s[1][:, :, :])
            for i in range(KT):
                split_lo(1 + i, (1 + i) % RING, wq_s[0][:, i, :], wq_s[1][:, i, :])
            split_lo(5, 0, wv_s[0][:, :, :], wv_s[1][:, :, :])
            for m in range(5):
                rope_sin(0, m)
                rope_lo(0, m, 0)
            group(0, False)
            with pool.Fori(1, KV - 1) as g:
                group(g, False)
            group(KV - 1, True)
            bias(1)

        @block.scalar
        def _(act):
            wbv = w_base.rearrange("(c p) d -> p c d", p=P)
            for c in range(OUT // P):
                act.dma_start(raw[:, c, :], wbv[:, c, :]).then_inc(w_landed[c], 16)
            act.dma_start(raw[:, 4, :], lora_a.rearrange("e r d -> (e r) d")).then_inc(la_landed, 16)
            act.dma_start(rot[0:EXPERTS, 1, :], w_router).then_inc(la_landed, 16)
            lbv = rot[:, 0, :].rearrange("p (c e r) -> p c e r", c=OUT // P, e=EXPERTS)
            for c in range(OUT // P):
                act.dma_start(lbv[:, c, :, :], lora_b[:, c * P:(c + 1) * P, :].rearrange("e p r -> p e r")).then_inc(lbr_landed, 16)
            act.dma_start(b_stage, b_base.rearrange("(a n) -> a n", a=1)).then_inc(b_landed, 16)

            for d in range(KT):
                act.wait_ge(prep_tr, d + 1)
                nc.scalar.activation(wb[0][:, d, :], bank[d][:, :], ACT.Copy).then_inc(prep_hi, 1)
            act.wait_ge(prep_tr, 5)
            nc.scalar.activation(ar[0][:, :, 0:ER], bank[4][:, :].rearrange("p (t n) -> p t n", t=KT),
                                 ACT.Copy).then_inc(prep_hi, 1)
            act.wait_ge(prep_tr, 6)
            nc.scalar.activation(ar[0][:, :, ER:ARW], bank[5][:, 0:KT * EXPERTS].rearrange("p (t n) -> p t n", t=KT),
                                 ACT.Copy).then_inc(prep_hi, 1)
            act.wait_ge(prep_tr, 7)
            nc.scalar.activation(lb[0][:, :], bank[6][:, :], ACT.Copy).then_inc(prep_hi, 1)
            act.wait_ge(prep_tr, 8)
            nc.scalar.activation(half_bias[:, :], bank[7][:, :], ACT.Copy, scale=0.5).then_inc(prep_hi, 1)

            def x_hi(ln, t):
                i = NT * ln + t
                act.wait_ge(tr_done, i + 1)
                nc.scalar.activation(xnT[0][:, :, t * P:(t + 1) * P], A[i % 2][:, :].rearrange("p (c n) -> p c n", c=KT),
                                     ACT.Copy).then_inc(xhi_done, 1)

            def ht_hi(f, pr):
                p = 4 * f + pr
                act.wait_ge(ht_done, p + 1)
                wait(act, out_done, NT * f + 2 * (pr - 1))
                nc.scalar.activation(oT[0][:, pr % 2, 0, 0:2, :], A[0][:, 0:2 * P].rearrange("p (i n) -> p i n", i=2),
                                     ACT.Copy).then_inc(hthi_done, 1)

            def ffn(f):
                for pr in range(NT // 2):
                    p = 4 * f + pr
                    x_hi(2 * f, 2 * pr)
                    x_hi(2 * f, 2 * pr + 1)
                    if pr:
                        ht_hi(f, pr - 1)
                    act.wait_ge(esub_done, p + 1)
                    if p == 0:
                        act.wait_ge(preset, 3)
                    nc.scalar.activation(ebuf[:, pr % 2, :, 0:EXPERTS], esub[:, :, :], ACT.Exp).then_inc(e_done, 1)
                ht_hi(f, NT // 2 - 1)

            def split_hi(n, slot, count, dst):
                act.wait_ge(raw_landed[slot], 16 * count)
                src = raw[:, slot, :]
                if len(dst.shape) == 3:
                    src = src.rearrange("p (t n) -> p t n", t=KT)
                nc.scalar.activation(dst, src, ACT.Copy).then_inc(conv_hi, 1)

            def weights(g, hf, s, last):
                def count(off):
                    return 2 * g + (6 + off) // RING + 1
                if hf == 0 and s in (4, 5):
                    for i in (2 * (s - 4), 2 * (s - 4) + 1):
                        wait(act, c_done, 8 * g)
                        split_hi(wo_pos(g, i), (6 + i) % RING, count(i), wo_s[0][:, i, :])
                if hf == 0 and s == 6 and not last:
                    act.wait_ge(a_done, 6 * (2 * g + 1) + 1)
                    split_hi(wk_pos(g + 1), (6 + 4) % RING, count(4), wk_s[0][:, :, :])
                if (hf, s) in ((0, 7), (1, 0)) and not last:
                    for i in ((0, 1) if hf == 0 else (2, 3)):
                        act.wait_ge(a_done, 6 * (2 * g + 1) + 5)
                        split_hi(wq_pos(g + 1, i), (11 + i) % RING, count(5 + i), wq_s[0][:, i, :])
                if hf == 1 and s == 2 and not last:
                    act.wait_ge(a_done, 6 * (2 * g + 1) + 6)
                    split_hi(wv_pos(g + 1), 15 % RING, count(9), wv_s[0][:, :, :])

            def rope_swap(j, m):
                r = 5 * j + m
                act.wait_ge(a_done, 6 * j + m + 1)
                wait(act, sum_done, {0: r, 1: r - 2}.get(m, r - 1))
                half = DH // 2
                for a, b in ((0, half), (half, 0)):
                    last = nc.scalar.activation(swap[a:a + half, m % 2, :], A[m % 2][b:b + half, :], ACT.Copy)
                    last.then_inc(swap_done, 1) if a else None

            def rope_hi(j, m, par):
                r = 5 * j + m
                hi = k[0][:, par, :] if m == 0 else q[0][:, par, m - 1, :]
                act.wait_ge(sum_done, r + 1)
                wait(act, s_done, SLOTS * (j - 1))
                nc.scalar.activation(hi, rot[:, m % 2, :], ACT.Copy).then_inc(qhi_done, 1)

            def v_hi(j, par):
                act.wait_ge(a_done, 6 * j + 6)
                wait(act, pv_done, 4 * (j - 1))
                nc.scalar.activation(v[0][:, par, :, :], A[1][:, :].rearrange("p (t n) -> p t n", t=HT),
                                     ACT.Copy).then_inc(vhi_done, 1)

            def softmax_exp(u, s):
                act.wait_ge(min_done, u + 1)
                wait(act, t_done, u - 1)
                for i, (lo, hi) in enumerate(((0, P), (P, 3 * P))):
                    last = nc.scalar.activation(prob[:, s % 2, lo:hi], sm[:, s % 2, lo:hi], ACT.Exp,
                                                bias=nmax[:, s % 2, i:i + 1], scale=-1.0,
                                                accum_out=rsum[:, s % 2, i:i + 1])
                last.then_inc(exp_done, 1)

            def p_hi(u, s, beta):
                act.wait_ge(t_done, u + 1)
                wait(act, pv_done, 2 * beta)
                nc.scalar.activation(pT[0][:, :, s % G, :], T[:, 0:3 * P].rearrange("p (c n) -> p c n", c=3),
                                     ACT.Copy).then_inc(pthi_done, 1)

            def o_hi(beta, par):
                for i in range(2):
                    act.wait_ge(pv_done, 2 * beta + i + 1)
                    wait(act, c_done, 2 * (beta - 1))
                    nc.scalar.activation(oT[0][:, par, i, :, :], O[i][:, :].rearrange("p (h n) -> p h n", h=G),
                                         ACT.Copy).then_inc(othi_done, 1)

            def group(g, first, last):
                for hf in range(2):
                    for s in range(SLOTS):
                        u, beta, b = 16 * g + 8 * hf + s, 4 * g + 2 * hf + s // G, s // G
                        start = first and hf == 0
                        softmax_exp(u, s)
                        m = ENDS.get(s) if not (last and hf == 1) else None
                        if m == 5:
                            v_hi(2 * g + hf + 1, 1 - hf)
                        elif m is not None:
                            rope_swap(2 * g + hf + 1, m)
                        if s % G == 1 and not (start and b == 0):
                            o_hi(beta - 1, (b + 1) % 2)
                        if not (start and s == 0):
                            p_hi(u - 1, s - 1, beta - (s % G == 0))
                        if m is not None and m < 5:
                            rope_hi(2 * g + hf + 1, m, 1 - hf)
                        weights(g, hf, s, last)

            ffn(0)
            for t in range(NT):
                x_hi(1, t)
            split_hi(0, 0, 1, wk_s[0][:, :, :])
            for i in range(KT):
                split_hi(1 + i, (1 + i) % RING, 1, wq_s[0][:, i, :])
            split_hi(5, 0, 2, wv_s[0][:, :, :])
            act.wait_ge(kept, 32)
            for m in range(5):
                rope_swap(0, m)
                rope_hi(0, m, 0)
            v_hi(0, 0)
            group(0, True, False)
            with act.Fori(1, KV - 1) as g:
                group(g, False, False)
            group(KV - 1, False, True)
            p_hi(16 * KV - 1, SLOTS - 1, 4 * KV - 1)
            o_hi(4 * KV - 1, 1)
            ffn(1)

        @block.vector
        def _(dve):
            steps = [0]

            def then(ins):
                steps[0] += 1
                ins.then_inc(step, 1)
                dve.wait_ge(step, steps[0])

            def norm_stats(ln, h):
                t0, t1 = 4 * h, 4 * h + 4
                for t in range(t0, t1):
                    if ln == 0 and t % 2 == 0:
                        dve.wait_ge(x_landed[t // 2], 16)
                    then(nc.vector.bn_stats(stats[:, t, :], x[:, t, :]))
                for t in range(t0, t1):
                    last = nc.vector.bn_aggr(mv[:, t, :], stats[:, t, :])
                then(last)
                vr, y, a, b = var[:, t0:t1], rstd[:, t0:t1], nt1[:, t0:t1], nt2[:, t0:t1]
                then(nc.vector.tensor_scalar(vr, mv[:, t0:t1, 1], EPS, None, ALU.add))
                then(nc.vector.tensor_scalar(a.bitcast(I32), vr.bitcast(I32), 1, None, ALU.logical_shift_right))
                then(nc.vector.tensor_scalar(y.bitcast(I32), a.bitcast(I32), -1.0, RSQRT_MAGIC, ALU.mult, ALU.add))
                for _ in range(NEWTON):
                    then(nc.vector.tensor_tensor(a, y, y, ALU.mult))
                    then(nc.vector.scalar_tensor_tensor(b, a, -0.5, vr, ALU.mult, ALU.mult))
                    then(nc.vector.scalar_tensor_tensor(y, b, 1.5, y, ALU.add, ALU.mult))

            def xn(ln, t):
                i = NT * ln + t
                wait(dve, tr_done, i - 1)
                nc.vector.tensor_scalar(swap[:, i % 2, :], x[:, t, :], mv[:, t, 0:1], rstd[:, t:t + 1],
                                        ALU.subtract, ALU.mult).then_inc(xn_done, 1)

            def x_lo(ln, t):
                i = NT * ln + t
                dve.wait_ge(xhi_done, i + 1)
                c = slice(t * P, (t + 1) * P)
                nc.vector.tensor_tensor(xnT[1][:, :, c], A[i % 2][:, :].rearrange("p (c n) -> p c n", c=KT),
                                        xnT[0][:, :, c].bitcast(F32), ALU.subtract).then_inc(xlo_done, 1)

            def router(f, pr):
                p = 4 * f + pr
                arv = S[pr % 2][:, 0:2 * ARW].rearrange("p (i c) -> p i c", i=2)
                lg = arv[:, :, ER:ARW]
                eb = ebuf[:, pr % 2, :, :]
                dve.wait_ge(ar_done, p + 1)
                for i in range(2):
                    last = nc.vector.max(top[:, i, :], lg[:, i, :])
                then(last)
                nc.vector.tensor_tensor(esub[:, :, :], lg, top[:, :, 0:1].broadcast_to([P, 2, EXPERTS]),
                                        ALU.subtract).then_inc(esub_done, 1)
                dve.wait_ge(e_done, p + 1)
                if p == 0:
                    dve.wait_ge(preset, 3)
                for i in range(2):
                    last = nc.vector.max(etop[:, i, :], eb[:, i, 0:EXPERTS])
                then(last)
                nc.vector.tensor_tensor(esum[:, :], etop[:, :, 0], etop[:, :, 1], ALU.add)
                then(nc.vector.tensor_copy(two[:, :, 0:2], etop[:, :, 0:2]))
                for i in range(2):
                    last = nc.vector.match_replace(rest[:, i, :], two[:, i, :], eb[:, i, :], 0.0)
                then(last)
                nc.vector.reciprocal(einv[:, :], esum[:, :])
                then(nc.vector.tensor_tensor(wgt[:, :, :], eb[:, :, 0:EXPERTS], rest[:, :, 0:EXPERTS], ALU.subtract))
                then(nc.vector.tensor_tensor(wgt[:, :, :], wgt[:, :, :],
                                             einv[:, :].unsqueeze(2).broadcast_to([P, 2, EXPERTS]), ALU.mult))
                wait(dve, ht_done, p)
                for i in range(2):
                    last = nc.vector.scalar_tensor_tensor(
                        sm[:, i, 0:ER].rearrange("p (e r) -> p e r", e=EXPERTS),
                        arv[:, i, 0:ER].rearrange("p (e r) -> p e r", e=EXPERTS), 2.0,
                        wgt[:, i, :].unsqueeze(2).broadcast_to([P, EXPERTS, RANK]), ALU.mult, ALU.mult)
                last.then_inc(hw_done, 1)

            def ht_lo(f, pr):
                p = 4 * f + pr
                dve.wait_ge(hthi_done, p + 1)
                nc.vector.tensor_tensor(oT[1][:, pr % 2, 0, 0:2, :], A[0][:, 0:2 * P].rearrange("p (i n) -> p i n", i=2),
                                        oT[0][:, pr % 2, 0, 0:2, :].bitcast(F32), ALU.subtract).then_inc(htlo_done, 1)

            def ffn_out(f, pr):
                for i in range(2):
                    t = 2 * pr + i
                    dve.wait_ge(out_done, NT * f + t + 1)
                    dve.wait_ge(biased, NT * f + t + 1)
                    nc.vector.scalar_tensor_tensor(x[:, t, :], OUTB[pr % 2][i][:, :], 0.5, x[:, t, :],
                                                   ALU.mult, ALU.add).then_inc(x_out, 1)

            def ffn(f):
                ln = 2 * f
                norm_stats(ln, 0)
                xn(ln, 0)
                xn(ln, 1)
                if f == 0:
                    prepare()
                for pr in range(NT // 2):
                    x_lo(ln, 2 * pr)
                    x_lo(ln, 2 * pr + 1)
                    if pr == 0:
                        norm_stats(ln, 1)
                    if pr < NT // 2 - 1:
                        xn(ln, 2 * pr + 2)
                        xn(ln, 2 * pr + 3)
                    if pr:
                        ht_lo(f, pr - 1)
                    router(f, pr)
                    if pr:
                        ffn_out(f, pr - 1)
                ht_lo(f, NT // 2 - 1)
                ffn_out(f, NT // 2 - 1)

            def prepare():
                for d in range(KT):
                    dve.wait_ge(prep_hi, d + 1)
                    nc.vector.tensor_tensor(wb[1][:, d, :], bank[d][:, :], wb[0][:, d, :].bitcast(F32),
                                            ALU.subtract).then_inc(prep_lo, 1)
                dve.wait_ge(prep_hi, 5)
                nc.vector.tensor_tensor(ar[1][:, :, 0:ER], bank[4][:, :].rearrange("p (t n) -> p t n", t=KT),
                                        ar[0][:, :, 0:ER].bitcast(F32), ALU.subtract).then_inc(prep_lo, 1)
                dve.wait_ge(prep_hi, 6)
                nc.vector.tensor_tensor(ar[1][:, :, ER:ARW], bank[5][:, 0:KT * EXPERTS].rearrange("p (t n) -> p t n", t=KT),
                                        ar[0][:, :, ER:ARW].bitcast(F32), ALU.subtract).then_inc(prep_lo, 1)
                dve.wait_ge(prep_hi, 7)
                nc.vector.tensor_tensor(lb[1][:, :], bank[6][:, :], lb[0][:, :].bitcast(F32),
                                        ALU.subtract).then_inc(prep_lo, 1)

            def rope_cos(j, m):
                r = 5 * j + m
                dve.wait_ge(swap_done, r + 1)
                wait(dve, qlo_done, {0: r, 1: r - 2}.get(m, r - 1))
                nc.vector.tensor_tensor(rot[:, m % 2, :].rearrange("p (b s) -> p b s", b=2),
                                        A[m % 2][:, :].rearrange("p (b s) -> p b s", b=2),
                                        rope[:, 0 if m == 0 else 2, :].unsqueeze(1).broadcast_to([P, 2, SEQ]),
                                        ALU.mult).then_inc(a_free, 1)

            def rope_sum(j, m):
                r = 5 * j + m
                dve.wait_ge(t2_done, r + 1)
                dve.wait_ge(a_free, 6 * j + m + 1)
                nc.vector.tensor_tensor(rot[:, m % 2, :], rot[:, m % 2, :], swap[:, m % 2, :],
                                        ALU.add).then_inc(sum_done, 1)

            def v_lo(j, par):
                dve.wait_ge(vhi_done, j + 1)
                nc.vector.tensor_tensor(v[1][:, par, :, :], A[1][:, :].rearrange("p (t n) -> p t n", t=HT),
                                        v[0][:, par, :, :].bitcast(F32), ALU.subtract).then_inc(a_free, 1)

            def softmax_min(u, s):
                dve.wait_ge(s_done, u + 1)
                wait(dve, exp_done, u - 1)
                nc.vector.memset(gate[:, :], 0.0)
                for i, (lo, hi) in enumerate(((0, P), (P, 3 * P))):
                    last = nc.vector.tensor_tensor_reduce(sm[:, s % 2, lo:hi], S[s % 2][:, lo:hi], mask[:, lo:hi],
                                                          1.0, FMAX, ALU.add, ALU.min, nmax[:, s % 2, i:i + 1])
                last.then_inc(min_done, 1)

            def softmax_norm(u, s):
                dve.wait_ge(exp_done, u + 1)
                nc.vector.reciprocal(rinv[:, s % 2, :], rsum[:, s % 2, :]).then_inc(rinv_done, 1)
                dve.wait_ge(rinv_done, u + 1)
                for i, (lo, hi) in enumerate(((0, P), (P, 3 * P))):
                    last = nc.vector.tensor_scalar(prob[:, s % 2, lo:hi], prob[:, s % 2, lo:hi],
                                                   rinv[:, s % 2, i:i + 1], None, ALU.mult)
                last.then_inc(norm_done, 1)

            def p_lo(u, s):
                dve.wait_ge(pthi_done, u + 1)
                nc.vector.tensor_tensor(pT[1][:, :, s % G, :], T[:, 0:3 * P].rearrange("p (c n) -> p c n", c=3),
                                        pT[0][:, :, s % G, :].bitcast(F32), ALU.subtract).then_inc(ptlo_done, 1)

            def o_lo(beta, par):
                for i in range(2):
                    dve.wait_ge(othi_done, 2 * beta + i + 1)
                    nc.vector.tensor_tensor(oT[1][:, par, i, :, :], O[i][:, :].rearrange("p (h n) -> p h n", h=G),
                                            oT[0][:, par, i, :, :].bitcast(F32), ALU.subtract).then_inc(otlo_done, 1)

            def x_add(beta, b, i):
                dve.wait_ge(c_done, 2 * beta + i + 1)
                wait(dve, x_added, 2 * beta + i)
                nc.vector.tensor_tensor(x[:, 2 * b + i, :], C[:, :], x[:, 2 * b + i, :], ALU.add).then_inc(x_added, 1)

            def group(g, first, last):
                for hf in range(2):
                    for s in range(SLOTS):
                        u, beta, b = 16 * g + 8 * hf + s, 4 * g + 2 * hf + s // G, 2 * hf + s // G
                        start = first and b == 0
                        softmax_min(u, s)
                        m = ENDS.get(s) if not (last and hf == 1) else None
                        if m == 5:
                            v_lo(2 * g + hf + 1, 1 - hf)
                        elif m is not None:
                            rope_cos(2 * g + hf + 1, m)
                        softmax_norm(u, s)
                        if s % G == 1 and not start:
                            o_lo(beta - 1, (b + 1) % 2)
                        if not (start and s == 0):
                            p_lo(u - 1, s - 1)
                        if m is not None and m < 5:
                            rope_sum(2 * g + hf + 1, m)
                        if s % G >= 2 and not start:
                            x_add(beta - 1, (b - 1) % BATCH, s % G - 2)

            ffn(0)
            norm_stats(1, 0)
            norm_stats(1, 1)
            xn(1, 0)
            xn(1, 1)
            for t in range(NT):
                x_lo(1, t)
                if t + 2 < NT:
                    xn(1, t + 2)
            dve.wait_ge(tables_landed, 32)
            for m in range(5):
                rope_cos(0, m)
                rope_sum(0, m)
            v_lo(0, 0)
            group(0, True, False)
            with dve.Fori(1, KV - 1) as g:
                group(g, False, False)
            group(KV - 1, False, True)
            p_lo(16 * KV - 1, SLOTS - 1)
            o_lo(4 * KV - 1, 1)
            x_add(4 * KV - 1, BATCH - 1, 0)
            x_add(4 * KV - 1, BATCH - 1, 1)
            ffn(1)

        @block.tensor
        def _(pe):
            mm, tp = nc.tensor.matmul, nc.tensor.transpose

            def prepare():
                pe.wait_ge(ident_landed, 16)
                for c in range(OUT // P):
                    pe.wait_ge(w_landed[c], 16)
                for d in range(KT):
                    for c in range(OUT // P):
                        last = tp(bank[d][:, c * P:(c + 1) * P], raw[:, c, d * P:(d + 1) * P], ident[:, :])
                    last.then_inc(prep_tr, 1)
                pe.wait_ge(la_landed, 32)
                for d in range(KT):
                    last = tp(bank[4][:, d * P:(d + 1) * P], raw[:, 4, d * P:(d + 1) * P], ident[:, :])
                last.then_inc(prep_tr, 1)
                for d in range(KT):
                    last = tp(bank[5][:, d * EXPERTS:(d + 1) * EXPERTS], rot[0:EXPERTS, 1, d * P:(d + 1) * P],
                              ident[0:EXPERTS, 0:EXPERTS])
                last.then_inc(prep_tr, 1)
                pe.wait_ge(lbr_landed, 16 * (OUT // P))
                for c in range(OUT // P):
                    last = tp(bank[6][:, c * P:(c + 1) * P], rot[:, 0, c * P:(c + 1) * P], ident[:, :])
                last.then_inc(prep_tr, 1)
                pe.wait_ge(b_landed, 16)
                pe.wait_ge(preset, 1)
                mm(bank[7][:, :], ones, b_stage, start=True, stop=True).then_inc(prep_tr, 1)

            def x_transpose(ln, t):
                i = NT * ln + t
                pe.wait_ge(xn_done, i + 1)
                wait(pe, xlo_done, i - 1)
                for c in range(KT):
                    last = tp(A[i % 2][:, c * P:(c + 1) * P], swap[:, i % 2, c * P:(c + 1) * P], ident[:, :])
                last.then_inc(tr_done, 1)

            def lora_router(f, pr):
                p = 4 * f + pr
                pe.wait_ge(xlo_done, NT * 2 * f + 2 * pr + 2)
                wait(pe, hw_done, p - 1)
                for i in range(2):
                    c = slice((2 * pr + i) * P, (2 * pr + i + 1) * P)
                    for n, (a, b) in enumerate(PASSES):
                        for d in range(KT):
                            last = mm(S[pr % 2][:, i * ARW:(i + 1) * ARW], xnT[a][:, d, c], ar[b][:, d, :],
                                      start=(n == 0 and d == 0), stop=(n == 2 and d == KT - 1))
                last.then_inc(ar_done, 1)

            def dense(f, pr):
                if pr >= 2:
                    pe.wait_ge(x_out, NT * f + 2 * pr - 2)
                for i in range(2):
                    c = slice((2 * pr + i) * P, (2 * pr + i + 1) * P)
                    for n, (a, b) in enumerate(PASSES):
                        for d in range(KT):
                            mm(OUTB[pr % 2][i][:, :], xnT[a][:, d, c], wb[b][:, d, :],
                               start=(n == 0 and d == 0), stop=False)

            def h_transpose(f, pr):
                p = 4 * f + pr
                pe.wait_ge(hw_done, p + 1)
                pe.wait_ge(xlo_done, NT * 2 * f + min(NT, 2 * pr + 4))
                for i in range(2):
                    last = tp(A[0][:, i * P:(i + 1) * P], sm[:, i, 0:ER], ident[:, :])
                last.then_inc(ht_done, 1)

            def lora_out(f, pr):
                pe.wait_ge(htlo_done, 4 * f + pr + 1)
                for i in range(2):
                    for n, (a, b) in enumerate(PASSES):
                        last = mm(OUTB[pr % 2][i][:, :], oT[a][:, pr % 2, 0, i, :], lb[b][:, :],
                                  start=False, stop=(n == 2))
                    last.then_inc(out_done, 1)

            def ffn(f):
                if f == 0:
                    pe.wait_ge(prep_lo, 7)
                    pe.wait_ge(prep_hi, 8)
                x_transpose(2 * f, 0)
                x_transpose(2 * f, 1)
                if f == 1:
                    pe.wait_ge(refetched, 32)
                for pr in range(NT // 2):
                    lora_router(f, pr)
                    if pr:
                        lora_out(f, pr - 1)
                    if pr < NT // 2 - 1:
                        if pr:
                            pe.wait_ge(htlo_done, 4 * f + pr)
                        x_transpose(2 * f, 2 * pr + 2)
                        x_transpose(2 * f, 2 * pr + 3)
                    dense(f, pr)
                    h_transpose(f, pr)
                lora_out(f, NT // 2 - 1)

            def project(j, hf, lo, hi, g):
                for n in range(lo, hi):
                    m, i = n // 12, n % 12
                    if i == 0:
                        wait(pe, a_free, 6 * j + m - 1)
                    if hf == 0 and i == 0:
                        if m == 0:
                            pe.wait_ge(conv_lo, wk_pos(g) + 1)
                        elif m == 1:
                            pe.wait_ge(conv_lo, wq_pos(g, KT - 1) + 1)
                        elif m == 5:
                            pe.wait_ge(conv_lo, wv_pos(g) + 1)
                    if m < 5:
                        a, b = PASSES[i // KT]
                        d = i % KT
                        w = wk_s[a][:, d, :] if m == 0 else wq_s[a][:, d, (m - 1) * DH:m * DH]
                        last = mm(A[m % 2][:, :], w, xnT[b][:, d, hf * HALF:(hf + 1) * HALF],
                                  start=(i == 0), stop=(i == 11))
                    else:
                        t, (a, b) = i // 3, PASSES[i % 3]
                        c = slice(hf * HALF + t * P, hf * HALF + (t + 1) * P)
                        for d in range(KT):
                            last = mm(A[1][:, t * DH:(t + 1) * DH], xnT[a][:, d, c], wv_s[b][:, d, :],
                                      start=(i % 3 == 0 and d == 0), stop=(i % 3 == 2 and d == KT - 1))
                    if i == 11:
                        last.then_inc(a_done, 1)

            def scores(u, s, j, hf):
                b, h = s // G, s % G
                pe.wait_ge(qlo_done, 5 * j + 2 + h)
                wait(pe, min_done, u - 1)
                for i, (lo, hi) in enumerate(((0, P), (P, 3 * P))):
                    for n, (a, c) in enumerate(PASSES):
                        last = mm(S[s % 2][:, lo:hi], q[a][:, hf, h, b * SEQ + i * P:b * SEQ + (i + 1) * P],
                                  k[c][:, hf, b * SEQ:b * SEQ + (i + 1) * P], start=(n == 0), stop=(n == 2))
                last.then_inc(s_done, 1)

            def p_transpose(u, s):
                pe.wait_ge(norm_done, u + 1)
                wait(pe, ptlo_done, u)
                for c in range(3):
                    last = tp(T[:, c * P:(c + 1) * P], prob[:, s % 2, c * P:(c + 1) * P], ident[:, :])
                last.then_inc(t_done, 1)

            def values(beta, par, b, j):
                pe.wait_ge(a_free, 6 * j + 6)
                pe.wait_ge(ptlo_done, 4 * beta + 4)
                wait(pe, otlo_done, 2 * beta)
                for i, blocks in enumerate((((0, 0),), ((1, 0), (2, 1)))):
                    todo = [(blk, kb, a, c) for blk, kb in blocks for a, c in PASSES]
                    for n, (blk, kb, a, c) in enumerate(todo):
                        last = mm(O[i][:, :], v[a][:, par, 2 * b + kb, :], pT[c][:, blk, :, :],
                                  start=(n == 0), stop=(n == len(todo) - 1))
                    last.then_inc(pv_done, 1)

            def out_project(beta, par, i, g):
                pe.wait_ge(conv_lo, wo_pos(g, G - 1) + 1)
                pe.wait_ge(otlo_done, 2 * beta + i + 1)
                wait(pe, x_added, 2 * beta + i)
                for h in range(G):
                    for n, (a, c) in enumerate(PASSES):
                        last = mm(C[:, :], oT[a][:, par, i, h, :], wo_s[c][:, h, :],
                                  start=(h == 0 and n == 0), stop=(h == G - 1 and n == 2))
                last.then_inc(c_done, 1)

            def group(g, first, last):
                for hf in range(2):
                    j = 2 * g + hf
                    for s in range(SLOTS):
                        u, beta, b = 16 * g + 8 * hf + s, 4 * g + 2 * hf + s // G, 2 * hf + s // G
                        start = first and b == 0
                        scores(u, s, j, hf)
                        if not (last and hf == 1):
                            project(j + 1, 1 - hf, CHUNK * s, CHUNK * (s + 1), g + hf)
                        prev_hf = ((b - 1) % BATCH) // 2
                        if s % G == 1 and not start:
                            values(beta - 1, prev_hf, (b - 1) % 2, j - (s < G))
                        if not (start and s == 0):
                            p_transpose(u - 1, s - 1)
                        if s % G >= 2 and not start:
                            out_project(beta - 1, (b - 1) % 2, s % G - 2, g if b else g - 1)

            prepare()
            ffn(0)
            for t in range(NT):
                if t == 0:
                    pe.wait_ge(htlo_done, 4)
                x_transpose(1, t)
            pe.wait_ge(xlo_done, 2 * NT)
            project(0, 0, 0, 6 * 12, 0)
            group(0, True, False)
            with pe.Fori(1, KV - 1) as g:
                group(g, False, False)
            group(KV - 1, False, True)
            p_transpose(16 * KV - 1, SLOTS - 1)
            values(4 * KV - 1, 1, 1, 2 * KV - 1)
            out_project(4 * KV - 1, 1, 0, KV - 1)
            out_project(4 * KV - 1, 1, 1, KV - 1)
            ffn(1)


_INS = ["L0_attn_x", "L0_attn_wq", "L0_attn_wk", "L0_attn_wv", "L0_attn_wo", "L0_ffn_W_base", "L0_ffn_b_base",
        "L0_ffn_W_router", "L0_ffn_lora_A", "L0_ffn_lora_B"]


def kernel(**inputs):
    import concourse.bacc as bacc
    from concourse.bass_utils import run_bass_kernel_spmd

    nc = bacc.Bacc("TRN2", target_bir_lowering=False, num_devices=1)
    arrays, args = {}, []
    for name in _INS:
        arrays[f"in_{name}"] = np.ascontiguousarray(inputs[name])
    for name, a in zip(("ident", "mask", "rope"), constants()):
        arrays[f"const_{name}"] = a
    for name, a in arrays.items():
        args.append(nc.dram_tensor(name, a.shape, mybir.dt.from_np(a.dtype), kind="ExternalInput").ap())
    args.append(nc.dram_tensor("out", (BATCH, SEQ, HID), F32, kind="ExternalOutput").ap())
    macaron(nc, *args)
    r = run_bass_kernel_spmd(nc, [arrays], core_ids=[0])
    return r.results[0]["out"]
```

```python
from contextlib import ExitStack

import numpy as np
import concourse.bass as bass
import concourse.mybir as mybir
from concourse.alu_op_type import AluOpType as ALU

F32 = mybir.dt.float32
F32R = mybir.dt.float32r
I32 = mybir.dt.int32
ACT = mybir.ActivationFunctionType

P = 128
BATCH, SEQ, HID = 4, 256, 512
TOK = BATCH * SEQ
NT = TOK // P
KT = HID // P
HEADS, KV, DH = 32, 8, 128
G = HEADS // KV
WINDOW = 128
EXPERTS, RANK, OUT = 8, 16, 512
ER = EXPERTS * RANK
ARW = ER + EXPERTS
EPS = 1e-5
SCALE = DH ** -0.5
THETA = 10000.0
HALF = 512
HT = HALF // P
FAR = 3.0e38
FMAX = 3.4e38
RSQRT_MAGIC = 1597463007.0
NEWTON = 3
RING = 5
SLOTS = 8
CHUNKS = (9, 9, 9, 9, 9, 9, 9, 9)
FIRST = [sum(CHUNKS[:s]) for s in range(SLOTS + 1)]
ENDS = {s: m for m in range(6) for s in range(SLOTS) if FIRST[s] < 12 * (m + 1) <= FIRST[s + 1]}
PASSES = ((0, 0), (0, 1), (1, 0))

assert WINDOW == P and SEQ == 2 * P and OUT == HID and G * DH == HID


def constants():
    ident = np.eye(P, dtype=np.float32)
    i, j = np.arange(P)[:, None], np.arange(P)[None, :]
    causal, past = j <= i, j > i
    mask = np.where(np.concatenate([causal, past, causal], axis=1), 0.0, FAR).astype(np.float32)
    half = DH // 2
    inv = np.power(np.float32(THETA), -np.arange(half, dtype=np.float32) / np.float32(half)).astype(np.float32)
    ang = (inv[:, None] * np.arange(SEQ, dtype=np.float32)[None, :]).astype(np.float32)
    cos, sin = np.cos(ang).astype(np.float32), np.sin(ang).astype(np.float32)
    cos = np.concatenate([cos, cos], axis=0)
    sin = np.concatenate([-sin, sin], axis=0)
    neg = np.float32(-SCALE)
    rope = np.stack([cos, sin, neg * cos, neg * sin], axis=1).astype(np.float32)
    return ident, mask, np.ascontiguousarray(rope)


def macaron(nc, x_in, wq, wk, wv, wo, w_base, b_base, w_router, lora_a, lora_b, ident_in, mask_in, rope_in, out):
    ctx = ExitStack()
    with ctx:
        def sb(name, shape, dt=F32):
            return ctx.enter_context(nc.sbuf_tensor(name, shape, dt))

        def sem(name):
            return ctx.enter_context(nc.semaphore(name))

        x = sb("x", [P, NT, HID])
        xnT = [sb(f"xnT_{s}", [P, KT, TOK], F32R) for s in ("hi", "lo")]
        ident = sb("ident", [P, P])
        mask = sb("mask", [P, 3 * P])
        rope = sb("rope", [P, 4, SEQ])
        half_bias = sb("half_bias", [P, OUT])
        ar = [sb(f"ar_{s}", [P, KT, ARW], F32R) for s in ("hi", "lo")]
        lb = [sb(f"lb_{s}", [P, OUT], F32R) for s in ("hi", "lo")]
        raw = sb("raw", [P, RING, HID])
        wq_s = [sb(f"wq_{s}", [P, KT, G * DH], F32R) for s in ("hi", "lo")]
        wk_s = [sb(f"wk_{s}", [P, KT, DH], F32R) for s in ("hi", "lo")]
        wv_s = [sb(f"wv_{s}", [P, KT, DH], F32R) for s in ("hi", "lo")]
        wo_s = [sb(f"wo_{s}", [P, G, HID], F32R) for s in ("hi", "lo")]
        q = [sb(f"q_{s}", [P, 2, G, HALF], F32R) for s in ("hi", "lo")]
        k_both = sb("k_hi_lo", [P, 2, 2, HALF], F32R)
        k = [k_both[:, s, :, :] for s in range(2)]
        v = [sb(f"v_{s}", [P, 2, HT, DH], F32R) for s in ("hi", "lo")]
        swap = sb("swap", [P, 2, HID])
        rot = sb("rot", [P, 2, HID])
        sm = sb("sm", [P, 2, 3 * P])
        prob = sb("prob", [P, 2, 3 * P])
        pT = [sb(f"pT_{s}", [P, 3, G, P], F32R) for s in ("hi", "lo")]
        oT = [sb(f"oT_{s}", [P, 2, 2, G, P], F32R) for s in ("hi", "lo")]
        nmax = sb("nmax", [P, 2, 2])
        part = sb("part", [P, P])
        gate = sb("gate", [P, 1])
        rsum = sb("rsum", [P, 2, 2])
        rinv = sb("rinv", [P, 2, 2])
        stats = sb("stats", [P, NT, 6])
        mv = sb("mv", [P, NT, 2])
        var = sb("var", [P, NT])
        rstd = sb("rstd", [P, NT])
        nt1 = sb("nt1", [P, NT])
        nt2 = sb("nt2", [P, NT])
        top = sb("top", [P, 2, 8])
        esub = sb("esub", [P, 2, 8])
        ebuf = sb("ebuf", [P, 2, 2, 16])
        etop = sb("etop", [P, 2, 8])
        two = sb("two", [P, 2, 8])
        rest = sb("rest", [P, 2, 16])
        esum = sb("esum", [P, 2])
        einv = sb("einv", [P, 2])
        wgt = sb("wgt", [P, 2, 8])
        ones_b = prob[:, :, :].rearrange("p a c -> p (a c)")
        b_stage, ones = ones_b[0:1, 0:OUT], ones_b[0:1, OUT:OUT + P]
        wb = [q[s][:, 0, :, :] for s in range(2)]

        wb_keep = [nc.dram_tensor(f"wb_keep_{s}", [P, KT, OUT], F32, kind="Internal").ap() for s in ("hi", "lo")]

        bank = [ctx.enter_context(nc.psum_tensor(f"bank{i}", [P, 512], F32)) for i in range(8)]
        A, S, T, O, C = bank[0:2], bank[2:4], bank[4], bank[5:7], bank[7]
        OUTB = [[bank[4], bank[5]], [bank[6], bank[7]]]

        ident_landed, tables_landed = sem("ident_landed"), sem("tables_landed")
        x_landed = [sem(f"x_landed{i}") for i in range(NT // 2)]
        w_landed = [sem(f"ffn_w_landed{i}") for i in range(4)]
        la_landed, lbr_landed, b_landed = sem("lora_a_landed"), sem("lora_b_landed"), sem("bias_landed")
        preset = sem("preset")
        prep_tr, prep_hi, prep_lo = sem("prep_transposed"), sem("prep_hi"), sem("prep_lo")
        kept, refetched = sem("wb_kept"), sem("wb_refetched")
        step = sem("dve_step")
        xn_done, tr_done, xhi_done, xlo_done = sem("xn_done"), sem("xT_done"), sem("xT_hi"), sem("xT_lo")
        biased = sem("bias_added")
        ar_done, esub_done, e_done, hw_done = sem("ar_done"), sem("esub_done"), sem("e_done"), sem("hw_done")
        ht_done, hthi_done, htlo_done = sem("hT_done"), sem("hT_hi"), sem("hT_lo")
        out_done, x_out = sem("ffn_out_done"), sem("ffn_x_done")
        stored = sem("stored")
        raw_landed = [sem(f"raw_landed{i}") for i in range(RING)]
        conv_hi, conv_lo, wo_lo = sem("w_hi_done"), sem("w_lo_done"), sem("wo_lo_done")
        a_done, a_free = sem("proj_done"), sem("proj_bank_read")
        vcopy_done, vt_done = sem("vT_copied"), sem("v_transposed")
        swap_done, t2_done, sum_done = sem("swap_done"), sem("sin_done"), sem("rope_sum_done")
        qhi_done, qlo_done, vhi_done = sem("qk_hi"), sem("qk_lo"), sem("v_hi")
        part_done = sem("part_scores_done")
        s_done, min_done, exp_done = sem("scores_done"), sem("min_done"), sem("exp_done")
        rinv_done, norm_done = sem("rinv_done"), sem("norm_done")
        t_done, pthi_done, ptlo_done = sem("pT_done"), sem("pT_hi"), sem("pT_lo")
        pv_done, othi_done, otlo_done = sem("pv_done"), sem("oT_hi"), sem("oT_lo")
        c_done, x_added = sem("wo_done"), sem("attn_x_done")

        def wait(eng, s, n):
            if not isinstance(n, int) or n > 0:
                eng.wait_ge(s, n)

        def wk_pos(g):
            return 10 * g

        def wq_pos(g, i):
            return 10 * g + 1 + i

        def wv_pos(g):
            return 10 * g + 5

        def wo_pos(g, i):
            return 10 * g + 6 + i

        WO_POOL = G // 2

        def wk_lo(g):
            return 8 * g + 1

        def wq_lo(g, i):
            return 8 * g + 2 + i

        def wv_lo(g):
            return 8 * g + 6

        def wo_lo_pool(g, i):
            return 8 * g + 7 + i

        def wo_lo_dve(g, i):
            return 2 * g + 1 + i - WO_POOL

        block = ctx.enter_context(nc.Block())

        @block.sync
        def _(sp):
            sp.dma_start(ident[:, :], ident_in).then_inc(ident_landed, 16)
            xv = x_in.rearrange("b (s p) d -> p (b s) d", p=P)
            for i in range(NT // 2):
                sp.dma_start(x[:, 2 * i:2 * i + 2, :], xv[:, 2 * i:2 * i + 2, :]).then_inc(x_landed[i], 16)
            sp.dma_start(mask[:, :], mask_in).then_inc(tables_landed, 16)
            sp.dma_start(rope[:, :, :], rope_in).then_inc(tables_landed, 16)

            def piece(slot, src):
                sp.dma_start(raw[:, slot, :] if len(src.shape) == 2 else
                             raw[:, slot, :].rearrange("p (t n) -> p t n", t=KT), src).then_inc(raw_landed[slot], 16)

            def wk_src(w, g):
                return w[:, bass.ds(g * DH, DH)].rearrange("(t p) n -> p t n", p=P)

            def wq_src(g, i):
                return wq[i * P:(i + 1) * P, bass.ds(g * (G * DH), G * DH)]

            def group(g, last):
                order = [("o", i) for i in range(G)]
                if not last:
                    order += [("k", 0)] + [("q", i) for i in range(KT)] + [("v", 0)]
                for kind, i in order:
                    if kind == "k":
                        sp.wait_ge(conv_lo, wv_lo(g))
                        off, src = 4, wk_src(wk, g + 1)
                    elif kind == "o":
                        sp.wait_ge(conv_lo, wq_lo(g, i))
                        off, src = i, wo[bass.ds(g * (G * DH) + i * DH, DH), :]
                    elif kind == "q":
                        if i < WO_POOL:
                            sp.wait_ge(conv_lo, wo_lo_pool(g, i))
                        else:
                            sp.wait_ge(wo_lo, wo_lo_dve(g, i))
                        off, src = 5 + i, wq_src(g + 1, i)
                    else:
                        sp.wait_ge(conv_lo, wk_lo(g + 1))
                        off, src = 9, wk_src(wv, g + 1)
                    piece((6 + off) % RING, src)

            sp.wait_ge(prep_tr, 5)
            piece(0, wk_src(wk, 0))
            for i in range(KT):
                piece((1 + i) % RING, wq_src(0, i))
            sp.wait_ge(conv_lo, wk_lo(0))
            piece(5 % RING, wk_src(wv, 0))
            sp.wait_ge(prep_lo, 4)
            for s in range(2):
                sp.dma_start(wb_keep[s], wb[s].bitcast(F32)).then_inc(kept, 16)
            group(0, False)
            with sp.Fori(1, KV - 1) as g:
                group(g, False)
            group(KV - 1, True)
            sp.wait_ge(kept, 32)
            sp.wait_ge(s_done, SLOTS * (2 * KV - 1))
            for s in range(2):
                sp.dma_start(wb[s].bitcast(F32), wb_keep[s]).then_inc(refetched, 16)
            ov = out.rearrange("b (s p) d -> p (b s) d", p=P)
            for t in range(NT):
                sp.wait_ge(x_out, NT + t + 1)
                sp.dma_start(ov[:, t, :], x[:, t, :]).then_inc(stored, 16)
            sp.wait_ge(stored, 16 * NT)

        @block.gpsimd
        def _(pool):
            nc.gpsimd.memset(ones, 1.0).then_inc(preset, 1)
            nc.gpsimd.memset(ebuf[:, :, :, :], -1.0).then_inc(preset, 1)
            nc.gpsimd.memset(two[:, :, :], -1.0).then_inc(preset, 1)

            def bias(f):
                ln = 2 * f
                if f == 0:
                    pool.wait_ge(prep_hi, 8)
                for t in range(NT):
                    pool.wait_ge(xn_done, NT * ln + t + 1)
                    nc.gpsimd.tensor_tensor(x[:, t, :], x[:, t, :], half_bias[:, :], ALU.add).then_inc(biased, 1)

            def split_lo(n, slot, hi, lo):
                pool.wait_ge(conv_hi, n + 1)
                src = raw[:, slot, :]
                if len(hi.shape) == 3:
                    src = src.rearrange("p (t n) -> p t n", t=KT)
                nc.gpsimd.tensor_tensor(lo, src, hi.bitcast(F32), ALU.subtract).then_inc(conv_lo, 1)

            def rope_sin(j, m):
                r = 5 * j + m
                w = swap[:, m % 2, :].rearrange("p (b s) -> p b s", b=2)
                tab = rope[:, 1 if m == 0 else 3, :].unsqueeze(1).broadcast_to([P, 2, SEQ])
                pool.wait_ge(swap_done, r + 1)
                nc.gpsimd.tensor_tensor(w, w, tab, ALU.mult).then_inc(t2_done, 1)

            def rope_sum(j, m):
                r = 5 * j + m
                pool.wait_ge(t2_done, r + 1)
                pool.wait_ge(a_free, 6 * j + m + 1)
                nc.gpsimd.tensor_tensor(rot[:, m % 2, :], rot[:, m % 2, :], swap[:, m % 2, :],
                                        ALU.add).then_inc(sum_done, 1)

            def rope_lo(j, m, par):
                r = 5 * j + m
                hi = k[0][:, par, :] if m == 0 else q[0][:, par, m - 1, :]
                lo = k[1][:, par, :] if m == 0 else q[1][:, par, m - 1, :]
                pool.wait_ge(qhi_done, r + 1)
                nc.gpsimd.tensor_tensor(lo, rot[:, m % 2, :], hi.bitcast(F32), ALU.subtract).then_inc(qlo_done, 1)

            def weights(g, hf, s, last):
                if hf == 0 and s == 4:
                    for i in range(WO_POOL):
                        split_lo(wo_pos(g, i), (6 + i) % RING, wo_s[0][:, i, :], wo_s[1][:, i, :])
                if hf == 0 and s == 5 and not last:
                    split_lo(wk_pos(g + 1), (6 + 4) % RING, wk_s[0][:, :, :], wk_s[1][:, :, :])
                if hf == 0 and s == 7 and not last:
                    for i in range(KT):
                        split_lo(wq_pos(g + 1, i), (6 + 5 + i) % RING, wq_s[0][:, i, :], wq_s[1][:, i, :])
                if hf == 1 and s == 2 and not last:
                    split_lo(wv_pos(g + 1), (6 + 9) % RING, wv_s[0][:, :, :], wv_s[1][:, :, :])

            def group(g, last):
                for hf in range(2):
                    for s in range(SLOTS):
                        split, m = (ENDS.get(c) if not (last and hf == 1) else None for c in (s - 1, s))
                        if m is not None and m < 5:
                            rope_sin(2 * g + hf + 1, m)
                            rope_sum(2 * g + hf + 1, m)
                        if split is not None and split < 5:
                            rope_lo(2 * g + hf + 1, split, 1 - hf)
                        weights(g, hf, s, last)

            bias(0)
            split_lo(0, 0, wk_s[0][:, :, :], wk_s[1][:, :, :])
            for i in range(KT):
                split_lo(1 + i, (1 + i) % RING, wq_s[0][:, i, :], wq_s[1][:, i, :])
            split_lo(5, 0, wv_s[0][:, :, :], wv_s[1][:, :, :])
            for m in range(6):
                if m < 5:
                    rope_sin(0, m)
                    rope_sum(0, m)
                if m:
                    rope_lo(0, m - 1, 0)
            group(0, False)
            with pool.Fori(1, KV - 1) as g:
                group(g, False)
            group(KV - 1, True)
            bias(1)

        @block.scalar
        def _(act):
            wbv = w_base.rearrange("(c p) d -> p c d", p=P)
            for c in range(OUT // P):
                act.dma_start(raw[:, c, :], wbv[:, c, :]).then_inc(w_landed[c], 16)
            act.dma_start(raw[:, 4, :], lora_a.rearrange("e r d -> (e r) d")).then_inc(la_landed, 16)
            act.dma_start(rot[0:EXPERTS, 1, :], w_router).then_inc(la_landed, 16)
            lbv = rot[:, 0, :].rearrange("p (c e r) -> p c e r", c=OUT // P, e=EXPERTS)
            for c in range(OUT // P):
                act.dma_start(lbv[:, c, :, :], lora_b[:, c * P:(c + 1) * P, :].rearrange("e p r -> p e r")).then_inc(lbr_landed, 16)
            act.dma_start(b_stage, b_base.rearrange("(a n) -> a n", a=1)).then_inc(b_landed, 16)

            for d in range(KT):
                act.wait_ge(prep_tr, d + 1)
                nc.scalar.activation(wb[0][:, d, :], bank[d][:, :], ACT.Copy).then_inc(prep_hi, 1)
            act.wait_ge(prep_tr, 5)
            nc.scalar.activation(ar[0][:, :, 0:ER], bank[4][:, :].rearrange("p (t n) -> p t n", t=KT),
                                 ACT.Copy).then_inc(prep_hi, 1)
            act.wait_ge(prep_tr, 6)
            nc.scalar.activation(ar[0][:, :, ER:ARW], bank[5][:, 0:KT * EXPERTS].rearrange("p (t n) -> p t n", t=KT),
                                 ACT.Copy).then_inc(prep_hi, 1)
            act.wait_ge(prep_tr, 7)
            nc.scalar.activation(lb[0][:, :], bank[6][:, :], ACT.Copy).then_inc(prep_hi, 1)
            act.wait_ge(prep_tr, 8)
            nc.scalar.activation(half_bias[:, :], bank[7][:, :], ACT.Copy, scale=0.5).then_inc(prep_hi, 1)

            def x_hi(ln, t):
                i = NT * ln + t
                act.wait_ge(tr_done, i + 1)
                nc.scalar.activation(xnT[0][:, :, t * P:(t + 1) * P], A[i % 2][:, :].rearrange("p (c n) -> p c n", c=KT),
                                     ACT.Copy).then_inc(xhi_done, 1)

            def ht_hi(f, pr):
                p = 4 * f + pr
                act.wait_ge(ht_done, p + 1)
                wait(act, out_done, NT * f + 2 * (pr - 1))
                nc.scalar.activation(oT[0][:, pr % 2, 0, 0:2, :], A[0][:, 0:2 * P].rearrange("p (i n) -> p i n", i=2),
                                     ACT.Copy).then_inc(hthi_done, 1)

            def ffn(f):
                for pr in range(NT // 2):
                    p = 4 * f + pr
                    x_hi(2 * f, 2 * pr)
                    x_hi(2 * f, 2 * pr + 1)
                    if pr:
                        ht_hi(f, pr - 1)
                    act.wait_ge(esub_done, p + 1)
                    if p == 0:
                        act.wait_ge(preset, 3)
                    nc.scalar.activation(ebuf[:, pr % 2, :, 0:EXPERTS], esub[:, :, :], ACT.Exp).then_inc(e_done, 1)
                ht_hi(f, NT // 2 - 1)

            def split_hi(n, slot, count, dst):
                act.wait_ge(raw_landed[slot], 16 * count)
                src = raw[:, slot, :]
                if len(dst.shape) == 3:
                    src = src.rearrange("p (t n) -> p t n", t=KT)
                nc.scalar.activation(dst, src, ACT.Copy).then_inc(conv_hi, 1)

            def weights(g, hf, s, last, part):
                def count(off):
                    return 2 * g + (6 + off) // RING + 1
                if hf == 0 and s == 4:
                    for i in part:
                        wait(act, c_done, 8 * g)
                        split_hi(wo_pos(g, i), (6 + i) % RING, count(i), wo_s[0][:, i, :])
                if hf == 0 and s == 5 and part[0] and not last:
                    act.wait_ge(a_done, 6 * (2 * g + 1) + 1)
                    split_hi(wk_pos(g + 1), (6 + 4) % RING, count(4), wk_s[0][:, :, :])
                if hf == 0 and s == 7 and not last:
                    for i in part:
                        act.wait_ge(a_done, 6 * (2 * g + 1) + 5)
                        split_hi(wq_pos(g + 1, i), (11 + i) % RING, count(5 + i), wq_s[0][:, i, :])
                if hf == 1 and s == 2 and part[0] and not last:
                    act.wait_ge(a_done, 6 * (2 * g + 1) + 6)
                    split_hi(wv_pos(g + 1), 15 % RING, count(9), wv_s[0][:, :, :])

            def rope_swap(j, m):
                r = 5 * j + m
                act.wait_ge(a_done, 6 * j + m + 1)
                wait(act, sum_done, {0: r, 1: r - 2}.get(m, r - 1))
                half = DH // 2
                for a, b in ((0, half), (half, 0)):
                    last = nc.scalar.activation(swap[a:a + half, m % 2, :], A[m % 2][b:b + half, :], ACT.Copy)
                    last.then_inc(swap_done, 1) if a else None

            def rope_hi(j, m, par):
                r = 5 * j + m
                hi = k[0][:, par, :] if m == 0 else q[0][:, par, m - 1, :]
                act.wait_ge(sum_done, r + 1)
                wait(act, s_done, SLOTS * (j - 1))
                nc.scalar.activation(hi, rot[:, m % 2, :], ACT.Copy).then_inc(qhi_done, 1)

            def v_copy(j):
                act.wait_ge(a_done, 6 * j + 6)
                act.wait_ge(sum_done, 5 * j + 4)
                nc.scalar.activation(swap[:, 1, :], A[1][:, :], ACT.Copy).then_inc(vcopy_done, 1)

            def v_hi(j, par):
                act.wait_ge(vt_done, j + 1)
                wait(act, pv_done, 4 * (j - 1))
                nc.scalar.activation(v[0][:, par, :, :], A[1][:, :].rearrange("p (t n) -> p t n", t=HT),
                                     ACT.Copy).then_inc(vhi_done, 1)

            def softmax_exp(u, s):
                act.wait_ge(min_done, u + 1)
                wait(act, t_done, u - 1)
                for i, (lo, hi) in enumerate(((0, P), (P, 3 * P))):
                    last = nc.scalar.activation(prob[:, s % 2, lo:hi], sm[:, s % 2, lo:hi], ACT.Exp,
                                                bias=nmax[:, s % 2, i:i + 1], scale=-1.0,
                                                accum_out=rsum[:, s % 2, i:i + 1])
                last.then_inc(exp_done, 1)

            def p_hi(u, s, beta):
                act.wait_ge(t_done, u + 1)
                wait(act, pv_done, 2 * beta)
                nc.scalar.activation(pT[0][:, :, s % G, :], T[:, 0:3 * P].rearrange("p (c n) -> p c n", c=3),
                                     ACT.Copy).then_inc(pthi_done, 1)

            def o_hi(beta, par):
                for i in range(2):
                    act.wait_ge(pv_done, 2 * beta + i + 1)
                    wait(act, c_done, 2 * (beta - 1))
                    nc.scalar.activation(oT[0][:, par, i, :, :], O[i][:, :].rearrange("p (h n) -> p h n", h=G),
                                         ACT.Copy).then_inc(othi_done, 1)

            def group(g, first, last):
                for hf in range(2):
                    for s in range(SLOTS):
                        u, beta, b = 16 * g + 8 * hf + s, 4 * g + 2 * hf + s // G, s // G
                        start = first and hf == 0
                        if s == 0:
                            v_hi(2 * g + hf, hf)
                        softmax_exp(u, s)
                        weights(g, hf, s, last, (0, 1))
                        split, m = (ENDS.get(c) if not (last and hf == 1) else None for c in (s - 1, s))
                        if m == 5:
                            v_copy(2 * g + hf + 1)
                        elif m is not None:
                            rope_swap(2 * g + hf + 1, m)
                        if s % G == 1 and not (start and b == 0):
                            o_hi(beta - 1, (b + 1) % 2)
                        if not (start and s == 0):
                            p_hi(u - 1, s - 1, beta - (s % G == 0))
                        if split is not None and split < 5:
                            rope_hi(2 * g + hf + 1, split, 1 - hf)
                        weights(g, hf, s, last, (2, 3))

            ffn(0)
            for t in range(NT):
                x_hi(1, t)
            split_hi(0, 0, 1, wk_s[0][:, :, :])
            for i in range(KT):
                split_hi(1 + i, (1 + i) % RING, 1, wq_s[0][:, i, :])
            split_hi(5, 0, 2, wv_s[0][:, :, :])
            act.wait_ge(kept, 32)
            for m in range(6):
                if m < 5:
                    rope_swap(0, m)
                if m:
                    rope_hi(0, m - 1, 0)
            v_copy(0)
            group(0, True, False)
            with act.Fori(1, KV - 1) as g:
                group(g, False, False)
            group(KV - 1, False, True)
            p_hi(16 * KV - 1, SLOTS - 1, 4 * KV - 1)
            o_hi(4 * KV - 1, 1)
            ffn(1)

        @block.vector
        def _(dve):
            steps = [0]

            def then(ins):
                steps[0] += 1
                ins.then_inc(step, 1)
                dve.wait_ge(step, steps[0])

            def norm_stats(ln, h):
                t0, t1 = 4 * h, 4 * h + 4
                for t in range(t0, t1):
                    if ln == 0 and t % 2 == 0:
                        dve.wait_ge(x_landed[t // 2], 16)
                    then(nc.vector.bn_stats(stats[:, t, :], x[:, t, :]))
                for t in range(t0, t1):
                    last = nc.vector.bn_aggr(mv[:, t, :], stats[:, t, :])
                then(last)
                vr, y, a, b = var[:, t0:t1], rstd[:, t0:t1], nt1[:, t0:t1], nt2[:, t0:t1]
                then(nc.vector.tensor_scalar(vr, mv[:, t0:t1, 1], EPS, None, ALU.add))
                then(nc.vector.tensor_scalar(a.bitcast(I32), vr.bitcast(I32), 1, None, ALU.logical_shift_right))
                then(nc.vector.tensor_scalar(y.bitcast(I32), a.bitcast(I32), -1.0, RSQRT_MAGIC, ALU.mult, ALU.add))
                for _ in range(NEWTON):
                    then(nc.vector.tensor_tensor(a, y, y, ALU.mult))
                    then(nc.vector.scalar_tensor_tensor(b, a, -0.5, vr, ALU.mult, ALU.mult))
                    then(nc.vector.scalar_tensor_tensor(y, b, 1.5, y, ALU.add, ALU.mult))

            def xn(ln, t):
                i = NT * ln + t
                wait(dve, tr_done, i - 1)
                nc.vector.tensor_scalar(swap[:, i % 2, :], x[:, t, :], mv[:, t, 0:1], rstd[:, t:t + 1],
                                        ALU.subtract, ALU.mult).then_inc(xn_done, 1)

            def x_lo(ln, t):
                i = NT * ln + t
                dve.wait_ge(xhi_done, i + 1)
                c = slice(t * P, (t + 1) * P)
                nc.vector.tensor_tensor(xnT[1][:, :, c], A[i % 2][:, :].rearrange("p (c n) -> p c n", c=KT),
                                        xnT[0][:, :, c].bitcast(F32), ALU.subtract).then_inc(xlo_done, 1)

            def router(f, pr):
                p = 4 * f + pr
                arv = S[pr % 2][:, 0:2 * ARW].rearrange("p (i c) -> p i c", i=2)
                lg = arv[:, :, ER:ARW]
                eb = ebuf[:, pr % 2, :, :]
                dve.wait_ge(ar_done, p + 1)
                for i in range(2):
                    last = nc.vector.max(top[:, i, :], lg[:, i, :])
                then(last)
                nc.vector.tensor_tensor(esub[:, :, :], lg, top[:, :, 0:1].broadcast_to([P, 2, EXPERTS]),
                                        ALU.subtract).then_inc(esub_done, 1)
                dve.wait_ge(e_done, p + 1)
                if p == 0:
                    dve.wait_ge(preset, 3)
                for i in range(2):
                    last = nc.vector.max(etop[:, i, :], eb[:, i, 0:EXPERTS])
                then(last)
                nc.vector.tensor_tensor(esum[:, :], etop[:, :, 0], etop[:, :, 1], ALU.add)
                then(nc.vector.tensor_copy(two[:, :, 0:2], etop[:, :, 0:2]))
                for i in range(2):
                    last = nc.vector.match_replace(rest[:, i, :], two[:, i, :], eb[:, i, :], 0.0)
                then(last)
                nc.vector.reciprocal(einv[:, :], esum[:, :])
                then(nc.vector.tensor_tensor(wgt[:, :, :], eb[:, :, 0:EXPERTS], rest[:, :, 0:EXPERTS], ALU.subtract))
                then(nc.vector.tensor_tensor(wgt[:, :, :], wgt[:, :, :],
                                             einv[:, :].unsqueeze(2).broadcast_to([P, 2, EXPERTS]), ALU.mult))
                wait(dve, ht_done, p)
                for i in range(2):
                    last = nc.vector.scalar_tensor_tensor(
                        sm[:, i, 0:ER].rearrange("p (e r) -> p e r", e=EXPERTS),
                        arv[:, i, 0:ER].rearrange("p (e r) -> p e r", e=EXPERTS), 2.0,
                        wgt[:, i, :].unsqueeze(2).broadcast_to([P, EXPERTS, RANK]), ALU.mult, ALU.mult)
                last.then_inc(hw_done, 1)

            def ht_lo(f, pr):
                p = 4 * f + pr
                dve.wait_ge(hthi_done, p + 1)
                nc.vector.tensor_tensor(oT[1][:, pr % 2, 0, 0:2, :], A[0][:, 0:2 * P].rearrange("p (i n) -> p i n", i=2),
                                        oT[0][:, pr % 2, 0, 0:2, :].bitcast(F32), ALU.subtract).then_inc(htlo_done, 1)

            def ffn_out(f, pr):
                for i in range(2):
                    t = 2 * pr + i
                    dve.wait_ge(out_done, NT * f + t + 1)
                    dve.wait_ge(biased, NT * f + t + 1)
                    nc.vector.scalar_tensor_tensor(x[:, t, :], OUTB[pr % 2][i][:, :], 0.5, x[:, t, :],
                                                   ALU.mult, ALU.add).then_inc(x_out, 1)

            def ffn(f):
                ln = 2 * f
                norm_stats(ln, 0)
                xn(ln, 0)
                xn(ln, 1)
                if f == 0:
                    prepare()
                for pr in range(NT // 2):
                    x_lo(ln, 2 * pr)
                    x_lo(ln, 2 * pr + 1)
                    if pr == 0:
                        norm_stats(ln, 1)
                    if pr < NT // 2 - 1:
                        xn(ln, 2 * pr + 2)
                        xn(ln, 2 * pr + 3)
                    if pr:
                        ht_lo(f, pr - 1)
                    router(f, pr)
                    if pr:
                        ffn_out(f, pr - 1)
                ht_lo(f, NT // 2 - 1)
                ffn_out(f, NT // 2 - 1)

            def prepare():
                for d in range(KT):
                    dve.wait_ge(prep_hi, d + 1)
                    nc.vector.tensor_tensor(wb[1][:, d, :], bank[d][:, :], wb[0][:, d, :].bitcast(F32),
                                            ALU.subtract).then_inc(prep_lo, 1)
                dve.wait_ge(prep_hi, 5)
                nc.vector.tensor_tensor(ar[1][:, :, 0:ER], bank[4][:, :].rearrange("p (t n) -> p t n", t=KT),
                                        ar[0][:, :, 0:ER].bitcast(F32), ALU.subtract).then_inc(prep_lo, 1)
                dve.wait_ge(prep_hi, 6)
                nc.vector.tensor_tensor(ar[1][:, :, ER:ARW], bank[5][:, 0:KT * EXPERTS].rearrange("p (t n) -> p t n", t=KT),
                                        ar[0][:, :, ER:ARW].bitcast(F32), ALU.subtract).then_inc(prep_lo, 1)
                dve.wait_ge(prep_hi, 7)
                nc.vector.tensor_tensor(lb[1][:, :], bank[6][:, :], lb[0][:, :].bitcast(F32),
                                        ALU.subtract).then_inc(prep_lo, 1)

            def rope_cos(j, m):
                r = 5 * j + m
                dve.wait_ge(swap_done, r + 1)
                wait(dve, qlo_done, {0: r, 1: r - 2}.get(m, r - 1))
                nc.vector.tensor_tensor(rot[:, m % 2, :].rearrange("p (b s) -> p b s", b=2),
                                        A[m % 2][:, :].rearrange("p (b s) -> p b s", b=2),
                                        rope[:, 0 if m == 0 else 2, :].unsqueeze(1).broadcast_to([P, 2, SEQ]),
                                        ALU.mult).then_inc(a_free, 1)

            def v_lo(j, par):
                dve.wait_ge(vhi_done, j + 1)
                nc.vector.tensor_tensor(v[1][:, par, :, :], A[1][:, :].rearrange("p (t n) -> p t n", t=HT),
                                        v[0][:, par, :, :].bitcast(F32), ALU.subtract).then_inc(a_free, 1)

            def softmax_min(u, s):
                dve.wait_ge(s_done, u + 1)
                wait(dve, exp_done, u - 1)
                sc = S[s % 2]
                nc.vector.tensor_tensor(part[:, :], sc[:, P:2 * P], mask[:, 0:P], ALU.add).then_inc(part_done, 1)
                nc.vector.tensor_tensor_reduce(sm[:, s % 2, P:3 * P], sc[:, 2 * P:4 * P], mask[:, P:3 * P],
                                               1.0, FMAX, ALU.add, ALU.min, nmax[:, s % 2, 1:2])
                dve.wait_ge(part_done, u + 1)
                nc.vector.memset(gate[:, :], 0.0)
                nc.vector.tensor_tensor_reduce(sm[:, s % 2, 0:P], sc[:, 0:P], part[:, :], 1.0, FMAX,
                                               ALU.add, ALU.min, nmax[:, s % 2, 0:1]).then_inc(min_done, 1)

            def softmax_norm(u, s):
                dve.wait_ge(exp_done, u + 1)
                nc.vector.reciprocal(rinv[:, s % 2, :], rsum[:, s % 2, :]).then_inc(rinv_done, 1)
                dve.wait_ge(rinv_done, u + 1)
                for i, (lo, hi) in enumerate(((0, P), (P, 3 * P))):
                    last = nc.vector.tensor_scalar(prob[:, s % 2, lo:hi], prob[:, s % 2, lo:hi],
                                                   rinv[:, s % 2, i:i + 1], None, ALU.mult)
                last.then_inc(norm_done, 1)

            def p_lo(u, s):
                dve.wait_ge(pthi_done, u + 1)
                nc.vector.tensor_tensor(pT[1][:, :, s % G, :], T[:, 0:3 * P].rearrange("p (c n) -> p c n", c=3),
                                        pT[0][:, :, s % G, :].bitcast(F32), ALU.subtract).then_inc(ptlo_done, 1)

            def o_lo(beta, par):
                for i in range(2):
                    dve.wait_ge(othi_done, 2 * beta + i + 1)
                    nc.vector.tensor_tensor(oT[1][:, par, i, :, :], O[i][:, :].rearrange("p (h n) -> p h n", h=G),
                                            oT[0][:, par, i, :, :].bitcast(F32), ALU.subtract).then_inc(otlo_done, 1)

            def x_add(beta, b, i):
                dve.wait_ge(c_done, 2 * beta + i + 1)
                wait(dve, x_added, 2 * beta + i)
                nc.vector.tensor_tensor(x[:, 2 * b + i, :], C[:, :], x[:, 2 * b + i, :], ALU.add).then_inc(x_added, 1)

            def wo_split(g):
                for i in range(WO_POOL, G):
                    dve.wait_ge(conv_hi, wo_pos(g, i) + 1)
                    nc.vector.tensor_tensor(wo_s[1][:, i, :], raw[:, (6 + i) % RING, :], wo_s[0][:, i, :].bitcast(F32),
                                            ALU.subtract).then_inc(wo_lo, 1)

            def group(g, first, last):
                for hf in range(2):
                    for s in range(SLOTS):
                        u, beta, b = 16 * g + 8 * hf + s, 4 * g + 2 * hf + s // G, 2 * hf + s // G
                        start = first and b == 0
                        softmax_min(u, s)
                        m = ENDS.get(s) if not (last and hf == 1) else None
                        if s == 0:
                            v_lo(2 * g + hf, hf)
                        if s % G == 3 and not start:
                            x_add(beta - 1, (b - 1) % BATCH, 0)
                        if s % G == 0 and not (first and b < 2):
                            x_add(beta - 2, (b - 2) % BATCH, 1)
                        softmax_norm(u, s)
                        if m is not None and m < 5:
                            rope_cos(2 * g + hf + 1, m)
                        if s % G == 1 and not start:
                            o_lo(beta - 1, (b + 1) % 2)
                        if not (start and s == 0):
                            p_lo(u - 1, s - 1)
                        if hf == 0 and s == 5:
                            wo_split(g)

            ffn(0)
            norm_stats(1, 0)
            norm_stats(1, 1)
            xn(1, 0)
            xn(1, 1)
            for t in range(NT):
                x_lo(1, t)
                if t + 2 < NT:
                    xn(1, t + 2)
            dve.wait_ge(tables_landed, 32)
            for m in range(5):
                rope_cos(0, m)
            group(0, True, False)
            with dve.Fori(1, KV - 1) as g:
                group(g, False, False)
            group(KV - 1, False, True)
            p_lo(16 * KV - 1, SLOTS - 1)
            o_lo(4 * KV - 1, 1)
            x_add(4 * KV - 2, BATCH - 2, 1)
            x_add(4 * KV - 1, BATCH - 1, 0)
            x_add(4 * KV - 1, BATCH - 1, 1)
            ffn(1)

        @block.tensor
        def _(pe):
            mm, tp = nc.tensor.matmul, nc.tensor.transpose

            def prepare():
                pe.wait_ge(ident_landed, 16)
                for c in range(OUT // P):
                    pe.wait_ge(w_landed[c], 16)
                for d in range(KT):
                    for c in range(OUT // P):
                        last = tp(bank[d][:, c * P:(c + 1) * P], raw[:, c, d * P:(d + 1) * P], ident[:, :])
                    last.then_inc(prep_tr, 1)
                pe.wait_ge(la_landed, 32)
                for d in range(KT):
                    last = tp(bank[4][:, d * P:(d + 1) * P], raw[:, 4, d * P:(d + 1) * P], ident[:, :])
                last.then_inc(prep_tr, 1)
                for d in range(KT):
                    last = tp(bank[5][:, d * EXPERTS:(d + 1) * EXPERTS], rot[0:EXPERTS, 1, d * P:(d + 1) * P],
                              ident[0:EXPERTS, 0:EXPERTS])
                last.then_inc(prep_tr, 1)
                pe.wait_ge(lbr_landed, 16 * (OUT // P))
                for c in range(OUT // P):
                    last = tp(bank[6][:, c * P:(c + 1) * P], rot[:, 0, c * P:(c + 1) * P], ident[:, :])
                last.then_inc(prep_tr, 1)
                pe.wait_ge(b_landed, 16)
                pe.wait_ge(preset, 1)
                mm(bank[7][:, :], ones, b_stage, start=True, stop=True).then_inc(prep_tr, 1)

            def x_transpose(ln, t):
                i = NT * ln + t
                pe.wait_ge(xn_done, i + 1)
                wait(pe, xlo_done, i - 1)
                for c in range(KT):
                    last = tp(A[i % 2][:, c * P:(c + 1) * P], swap[:, i % 2, c * P:(c + 1) * P], ident[:, :])
                last.then_inc(tr_done, 1)

            def lora_router(f, pr):
                p = 4 * f + pr
                pe.wait_ge(xlo_done, NT * 2 * f + 2 * pr + 2)
                wait(pe, hw_done, p - 1)
                for i in range(2):
                    c = slice((2 * pr + i) * P, (2 * pr + i + 1) * P)
                    for n, (a, b) in enumerate(PASSES):
                        for d in range(KT):
                            last = mm(S[pr % 2][:, i * ARW:(i + 1) * ARW], xnT[a][:, d, c], ar[b][:, d, :],
                                      start=(n == 0 and d == 0), stop=(n == 2 and d == KT - 1))
                last.then_inc(ar_done, 1)

            def dense(f, pr):
                if pr >= 2:
                    pe.wait_ge(x_out, NT * f + 2 * pr - 2)
                for i in range(2):
                    c = slice((2 * pr + i) * P, (2 * pr + i + 1) * P)
                    for n, (a, b) in enumerate(PASSES):
                        for d in range(KT):
                            mm(OUTB[pr % 2][i][:, :], xnT[a][:, d, c], wb[b][:, d, :],
                               start=(n == 0 and d == 0), stop=False)

            def h_transpose(f, pr):
                p = 4 * f + pr
                pe.wait_ge(hw_done, p + 1)
                pe.wait_ge(xlo_done, NT * 2 * f + min(NT, 2 * pr + 4))
                for i in range(2):
                    last = tp(A[0][:, i * P:(i + 1) * P], sm[:, i, 0:ER], ident[:, :])
                last.then_inc(ht_done, 1)

            def lora_out(f, pr):
                pe.wait_ge(htlo_done, 4 * f + pr + 1)
                for i in range(2):
                    for n, (a, b) in enumerate(PASSES):
                        last = mm(OUTB[pr % 2][i][:, :], oT[a][:, pr % 2, 0, i, :], lb[b][:, :],
                                  start=False, stop=(n == 2))
                    last.then_inc(out_done, 1)

            def ffn(f):
                if f == 0:
                    pe.wait_ge(prep_lo, 7)
                    pe.wait_ge(prep_hi, 8)
                x_transpose(2 * f, 0)
                x_transpose(2 * f, 1)
                if f == 1:
                    pe.wait_ge(refetched, 32)
                for pr in range(NT // 2):
                    lora_router(f, pr)
                    if pr:
                        lora_out(f, pr - 1)
                    if pr < NT // 2 - 1:
                        if pr:
                            pe.wait_ge(htlo_done, 4 * f + pr)
                        x_transpose(2 * f, 2 * pr + 2)
                        x_transpose(2 * f, 2 * pr + 3)
                    dense(f, pr)
                    h_transpose(f, pr)
                lora_out(f, NT // 2 - 1)

            def project(j, hf, lo, hi, g):
                for n in range(lo, hi):
                    m, i = n // 12, n % 12
                    if i == 0:
                        wait(pe, a_free, 6 * j + m - 1)
                    if hf == 0 and i == 0 and m in (0, 1, 5):
                        pe.wait_ge(conv_hi, {0: wk_pos(g), 1: wq_pos(g, KT - 1), 5: wv_pos(g)}[m] + 1)
                    if hf == 0 and i == 2 * KT and m in (0, 1, 5):
                        pe.wait_ge(conv_lo, {0: wk_lo(g), 1: wq_lo(g, KT - 1), 5: wv_lo(g)}[m])
                    a, b = PASSES[i // KT]
                    d = i % KT
                    w = wk_s[a][:, d, :] if m == 0 else wv_s[a][:, d, :] if m == 5 else wq_s[a][:, d, (m - 1) * DH:m * DH]
                    last = mm(A[m % 2][:, :], w, xnT[b][:, d, hf * HALF:(hf + 1) * HALF],
                              start=(i == 0), stop=(i == 11))
                    if i == 11:
                        last.then_inc(a_done, 1)

            def v_transpose(j):
                pe.wait_ge(vcopy_done, j + 1)
                for t in range(HT):
                    last = tp(A[1][:, t * DH:(t + 1) * DH], swap[:, 1, t * P:(t + 1) * P], ident[:, :])
                last.then_inc(vt_done, 1)

            def scores(u, s, j, hf):
                b, h = s // G, s % G
                pe.wait_ge(qlo_done, 5 * j + 2 + h)
                wait(pe, min_done, u - 1)
                q0, q1 = (slice(b * SEQ + i * P, b * SEQ + (i + 1) * P) for i in range(2))
                mm(S[s % 2][:, 0:2 * P], q[0][:, hf, h, q0], k_both[:, :, hf, q0], start=True, stop=False)
                mm(S[s % 2][:, 0:P], q[1][:, hf, h, q0], k[0][:, hf, q0], start=False, stop=True)
                for n, (a, c) in enumerate(PASSES):
                    last = mm(S[s % 2][:, 2 * P:4 * P], q[a][:, hf, h, q1], k[c][:, hf, b * SEQ:(b + 1) * SEQ],
                              start=(n == 0), stop=(n == 2))
                last.then_inc(s_done, 1)

            def p_transpose(u, s):
                pe.wait_ge(norm_done, u + 1)
                wait(pe, ptlo_done, u)
                for c in range(3):
                    last = tp(T[:, c * P:(c + 1) * P], prob[:, s % 2, c * P:(c + 1) * P], ident[:, :])
                last.then_inc(t_done, 1)

            def values(beta, par, b, j):
                pe.wait_ge(a_free, 6 * j + 6)
                pe.wait_ge(pthi_done, 4 * beta + 4)
                wait(pe, otlo_done, 2 * beta)
                blocks = ((0, 0, 0), (1, 1, 0), (1, 2, 1))
                for n, (a, c) in enumerate(((0, 0), (1, 0), (0, 1))):
                    if c:
                        pe.wait_ge(ptlo_done, 4 * beta + 4)
                    for i, blk, kb in blocks:
                        last = mm(O[i][:, :], v[a][:, par, 2 * b + kb, :], pT[c][:, blk, :, :],
                                  start=(n == 0 and blk < 2), stop=(n == 2 and blk != 1))
                        if n == 2 and blk != 1:
                            last.then_inc(pv_done, 1)

            def out_project(beta, par, i, g):
                pe.wait_ge(conv_hi, wo_pos(g, G - 1) + 1)
                pe.wait_ge(othi_done, 2 * beta + i + 1)
                wait(pe, x_added, 2 * beta + i)
                for n, (a, c) in enumerate(((0, 0), (0, 1), (1, 0))):
                    if c:
                        pe.wait_ge(conv_lo, wo_lo_pool(g, WO_POOL - 1))
                        pe.wait_ge(wo_lo, wo_lo_dve(g, G - 1))
                    if a:
                        pe.wait_ge(otlo_done, 2 * beta + i + 1)
                    for h in range(G):
                        last = mm(C[:, :], oT[a][:, par, i, h, :], wo_s[c][:, h, :],
                                  start=(h == 0 and n == 0), stop=(h == G - 1 and n == 2))
                last.then_inc(c_done, 1)

            def group(g, first, last):
                for hf in range(2):
                    j = 2 * g + hf
                    for s in range(SLOTS):
                        u, beta, b = 16 * g + 8 * hf + s, 4 * g + 2 * hf + s // G, 2 * hf + s // G
                        start = first and b == 0
                        scores(u, s, j, hf)
                        if s == 0:
                            v_transpose(j)
                        if not (last and hf == 1):
                            project(j + 1, 1 - hf, FIRST[s], FIRST[s + 1], g + hf)
                        prev_hf = ((b - 1) % BATCH) // 2
                        if s % G == 1 and not start:
                            values(beta - 1, prev_hf, (b - 1) % 2, j - (s < G))
                        if not (start and s == 0):
                            p_transpose(u - 1, s - 1)
                        if s % G >= 2 and not start:
                            out_project(beta - 1, (b - 1) % 2, s % G - 2, g if b else g - 1)

            prepare()
            ffn(0)
            for t in range(NT):
                if t == 0:
                    pe.wait_ge(htlo_done, 4)
                x_transpose(1, t)
            pe.wait_ge(xlo_done, 2 * NT)
            project(0, 0, 0, 6 * 12, 0)
            group(0, True, False)
            with pe.Fori(1, KV - 1) as g:
                group(g, False, False)
            group(KV - 1, False, True)
            p_transpose(16 * KV - 1, SLOTS - 1)
            values(4 * KV - 1, 1, 1, 2 * KV - 1)
            out_project(4 * KV - 1, 1, 0, KV - 1)
            out_project(4 * KV - 1, 1, 1, KV - 1)
            ffn(1)


_INS = ["L0_attn_x", "L0_attn_wq", "L0_attn_wk", "L0_attn_wv", "L0_attn_wo", "L0_ffn_W_base", "L0_ffn_b_base",
        "L0_ffn_W_router", "L0_ffn_lora_A", "L0_ffn_lora_B"]


def kernel(**inputs):
    import concourse.bacc as bacc
    from concourse.bass_utils import run_bass_kernel_spmd

    nc = bacc.Bacc("TRN2", target_bir_lowering=False, num_devices=1)
    arrays, args = {}, []
    for name in _INS:
        arrays[f"in_{name}"] = np.ascontiguousarray(inputs[name])
    for name, a in zip(("ident", "mask", "rope"), constants()):
        arrays[f"const_{name}"] = a
    for name, a in arrays.items():
        args.append(nc.dram_tensor(name, a.shape, mybir.dt.from_np(a.dtype), kind="ExternalInput").ap())
    args.append(nc.dram_tensor("out", (BATCH, SEQ, HID), F32, kind="ExternalOutput").ap())
    macaron(nc, *args)
    r = run_bass_kernel_spmd(nc, [arrays], core_ids=[0])
    return r.results[0]["out"]
```

```python
from contextlib import ExitStack

import numpy as np
import concourse.bass as bass
import concourse.mybir as mybir
from concourse.alu_op_type import AluOpType as ALU

F32 = mybir.dt.float32
F32R = mybir.dt.float32r
I32 = mybir.dt.int32
ACT = mybir.ActivationFunctionType

P = 128
BATCH, SEQ, HID = 4, 256, 512
TOK = BATCH * SEQ
NT = TOK // P
KT = HID // P
HEADS, KV, DH = 32, 8, 128
G = HEADS // KV
WINDOW = 128
EXPERTS, RANK, OUT = 8, 16, 512
ER = EXPERTS * RANK
ARW = ER + EXPERTS
EPS = 1e-5
SCALE = DH ** -0.5
THETA = 10000.0
HALF = 512
HT = HALF // P
FAR = 3.0e38
FMAX = 3.4e38
RSQRT_MAGIC = 1597463007.0
NEWTON = 3
WARM = 7
RING = 5
SLOTS = 8
CHUNKS = (9,) * SLOTS
FIRST = [sum(CHUNKS[:s]) for s in range(SLOTS + 1)]
ENDS = {s: m for m in range(6) for s in range(SLOTS) if FIRST[s] < 12 * (m + 1) <= FIRST[s + 1]}
PASSES = ((0, 0), (0, 1), (1, 0))

assert WINDOW == P and SEQ == 2 * P and OUT == HID and G * DH == HID


def constants():
    ident = np.eye(P, dtype=np.float32)
    i, j = np.arange(P)[:, None], np.arange(P)[None, :]
    causal, past = j <= i, j > i
    mask = np.where(np.concatenate([causal, past, causal], axis=1), 0.0, FAR).astype(np.float32)
    side = np.stack([~causal.T, causal.T], axis=1).astype(np.float32)
    half = DH // 2
    inv = np.power(np.float32(THETA), -np.arange(half, dtype=np.float32) / np.float32(half)).astype(np.float32)
    ang = (inv[:, None] * np.arange(SEQ, dtype=np.float32)[None, :]).astype(np.float32)
    cos, sin = np.cos(ang).astype(np.float32), np.sin(ang).astype(np.float32)
    cos = np.concatenate([cos, cos], axis=0)
    sin = np.concatenate([-sin, sin], axis=0)
    neg = np.float32(-SCALE)
    rope = np.stack([cos, sin, neg * cos, neg * sin], axis=1).astype(np.float32)
    return ident, mask, np.ascontiguousarray(side), np.ascontiguousarray(rope)


def macaron(nc, x_in, wq, wk, wv, wo, w_base, b_base, w_router, lora_a, lora_b, ident_in, mask_in, side_in, rope_in, out):
    ctx = ExitStack()
    with ctx:
        def sb(name, shape, dt=F32):
            return ctx.enter_context(nc.sbuf_tensor(name, shape, dt))

        def sem(name):
            return ctx.enter_context(nc.semaphore(name))

        x = sb("x", [P, NT, HID])
        xnT = [sb(f"xnT_{s}", [P, KT, TOK], F32R) for s in ("hi", "lo")]
        ident = sb("ident", [P, P])
        mask = sb("mask", [P, 3 * P])
        side = sb("side", [P, 2, P])
        rope = sb("rope", [P, 4, SEQ])
        half_bias = sb("half_bias", [P, OUT])
        ar_both = sb("ar_hi_lo", [P, KT, 2, ARW], F32R)
        ar = [ar_both[:, :, s, :] for s in range(2)]
        lb = [sb(f"lb_{s}", [P, OUT], F32R) for s in ("hi", "lo")]
        raw = sb("raw", [P, RING, HID])
        wq_s = [sb(f"wq_{s}", [P, KT, G * DH], F32R) for s in ("hi", "lo")]
        wk_s = [sb(f"wk_{s}", [P, KT, DH], F32R) for s in ("hi", "lo")]
        wv_s = [sb(f"wv_{s}", [P, KT, DH], F32R) for s in ("hi", "lo")]
        wo_s = [sb(f"wo_{s}", [P, G, HID], F32R) for s in ("hi", "lo")]
        q = [sb(f"q_{s}", [P, 2, G, HALF], F32R) for s in ("hi", "lo")]
        k_both = sb("k_hi_lo", [P, 2, 2, HALF], F32R)
        k = [k_both[:, s, :, :] for s in range(2)]
        v = [sb(f"v_{s}", [P, 2, HT, DH], F32R) for s in ("hi", "lo")]
        swap = sb("swap", [P, 2, HID])
        rot = sb("rot", [P, 2, HID])
        sm = sb("sm", [P, 2, 3 * P])
        prob = sb("prob", [P, 2, 3 * P])
        pT_both = sb("pT_hi_lo", [P, 2, 3, G, P], F32R)
        pT = [pT_both[:, s, :, :, :] for s in range(2)]
        oT = [sb(f"oT_{s}", [P, 2, 2, G, P], F32R) for s in ("hi", "lo")]
        nmax = sb("nmax", [P, 2, 2])
        gate = sb("gate", [P, 1])
        gate_pool = sb("gate_pool", [P, 1])
        rsum = sb("rsum", [P, 2, 2])
        rinv = sb("rinv", [P, 2, 2])
        stats = sb("stats", [P, NT, 6])
        mv = sb("mv", [P, NT, 2])
        var = sb("var", [P, NT])
        rstd = sb("rstd", [P, NT])
        nt1 = sb("nt1", [P, NT])
        nt2 = sb("nt2", [P, NT])
        top = sb("top", [P, 2, 8])
        ar_part = sb("ar_part", [P, 2, ARW])
        logits = sb("logits", [P, 2, EXPERTS])
        esub = sb("esub", [P, 2, 8])
        ebuf = sb("ebuf", [P, 2, 2, 16])
        etop = sb("etop", [P, 2, 8])
        two = sb("two", [P, 2, 8])
        rest = sb("rest", [P, 2, 16])
        esum = sb("esum", [P, 2])
        einv = sb("einv", [P, 2])
        wgt = sb("wgt", [P, 2, 8])
        ones_b = prob[:, :, :].rearrange("p a c -> p (a c)")
        b_stage, ones = ones_b[0:1, 0:OUT], ones_b[0:1, OUT:OUT + P]
        wb = [q[s][:, 0, :, :] for s in range(2)]

        wb_keep = [nc.dram_tensor(f"wb_keep_{s}", [P, KT, OUT], F32, kind="Internal").ap() for s in ("hi", "lo")]

        bank = [ctx.enter_context(nc.psum_tensor(f"bank{i}", [P, 512], F32)) for i in range(8)]
        A, S, T, O, C = bank[0:2], bank[2:4], bank[4], bank[5:7], bank[7]
        OUTB = [[[bank[4], bank[5]], [bank[6], bank[7]]], [[bank[0], bank[1]], [bank[6], bank[7]]]]

        def ht_bank(f, pr):
            if f == 0:
                return bank[0] if pr == 2 else bank[2]
            return bank[4] if pr else bank[3]

        def xt_bank(ln, t):
            if ln == 1 and 4 <= t < 6:
                return S[t % 2]
            if ln == 1 and t >= 6 or ln == 2 and t >= 2:
                return bank[4 + t % 2]
            return A[t % 2]

        def xn_buf(ln, t):
            if ln == 1:
                return (prob, sm)[t % 2][:, :, P:3 * P]
            return swap[:, t % 2, :].rearrange("p (a n) -> p a n", a=2)

        ident_landed, tables_landed = sem("ident_landed"), sem("tables_landed")
        x_landed = [sem(f"x_landed{i}") for i in range(NT // 2)]
        w_landed = [sem(f"ffn_w_landed{i}") for i in range(4)]
        la_landed, lbr_landed, b_landed = sem("lora_a_landed"), sem("lora_b_landed"), sem("bias_landed")
        preset, warm_ready = sem("preset"), sem("warm_up_ready")
        prep_tr, prep_hi, prep_lo = sem("prep_transposed"), sem("prep_hi"), sem("prep_lo")
        kept, refetched = sem("wb_kept"), sem("wb_refetched")
        step, aggr = sem("dve_step"), sem("mean_var_done")
        pool_step, rstd_done = sem("pool_step"), sem("pool_rstd_done")
        xn_done, tr_done, xhi_done, xlo_done = sem("xn_done"), sem("xT_done"), sem("xT_hi"), sem("xT_lo")
        biased = sem("bias_added")
        ar_copied = sem("ar_part_copied")
        ar_done, esub_done, e_done, hw_done = sem("ar_done"), sem("esub_done"), sem("e_done"), sem("hw_done")
        ht_done, hthi_done, htlo_done = sem("hT_done"), sem("hT_hi"), sem("hT_lo")
        out_done, x_out = sem("ffn_out_done"), sem("ffn_x_done")
        stored = sem("stored")
        raw_landed = [sem(f"raw_landed{i}") for i in range(RING)]
        conv_hi, conv_lo, wo_lo = sem("w_hi_done"), sem("w_lo_done"), sem("wo_lo_done")
        a_done, a_free = sem("proj_done"), sem("proj_bank_read")
        vcopy_done, vt_done = sem("vT_copied"), sem("v_transposed")
        swap_done, t2_done, sum_done = sem("swap_done"), sem("sin_done"), sem("rope_sum_done")
        qhi_done, qlo_done, vhi_done = sem("qk_hi"), sem("qk_lo"), sem("v_hi")
        part_done = sem("part_scores_done")
        s_done, min_done, exp_done = sem("scores_done"), sem("min_done"), sem("exp_done")
        rinv_done, norm_done = sem("rinv_done"), sem("norm_done")
        parted = sem("pT_parted")
        t_done, pthi_done, ptlo_done = sem("pT_done"), sem("pT_hi"), sem("pT_lo")
        pv_done, othi_done, otlo_done = sem("pv_done"), sem("oT_hi"), sem("oT_lo")
        c_done, x_added = sem("wo_done"), sem("attn_x_done")

        def wait(eng, s, n):
            if not isinstance(n, int) or n > 0:
                eng.wait_ge(s, n)

        def wk_pos(g):
            return 10 * g

        def wq_pos(g, i):
            return 10 * g + 1 + i

        def wv_pos(g):
            return 10 * g + 5

        def wo_pos(g, i):
            return 10 * g + 6 + i

        WO_POOL = G // 2

        def wk_lo(g):
            return 8 * g + 1

        def wq_lo(g, i):
            return 8 * g + 2 + i

        def wv_lo(g):
            return 8 * g + 6

        def wo_lo_pool(g, i):
            return 8 * g + 7 + i

        def wo_lo_dve(g, i):
            return 2 * g + 1 + i - WO_POOL

        def rstd_steps(engine, then, t0, t1):
            vr, y, a, b = var[:, t0:t1], rstd[:, t0:t1], nt1[:, t0:t1], nt2[:, t0:t1]
            then(engine.tensor_scalar(vr, mv[:, t0:t1, 1], EPS, None, ALU.add))
            then(engine.tensor_scalar(y.bitcast(I32), vr.bitcast(I32), -0.5, RSQRT_MAGIC, ALU.mult, ALU.add))
            for _ in range(NEWTON):
                then(engine.tensor_tensor(a, y, y, ALU.mult))
                if engine is nc.vector:
                    then(engine.scalar_tensor_tensor(b, a, -0.5, vr, ALU.mult, ALU.mult))
                    then(engine.scalar_tensor_tensor(y, b, 1.5, y, ALU.add, ALU.mult))
                else:
                    then(engine.tensor_tensor(b, a, vr, ALU.mult))
                    then(engine.tensor_scalar(b, b, -0.5, 1.5, ALU.mult, ALU.add))
                    then(engine.tensor_tensor(y, y, b, ALU.mult))

        block = ctx.enter_context(nc.Block())

        @block.sync
        def _(sp):
            sp.dma_start(ident[:, :], ident_in).then_inc(ident_landed, 16)
            xv = x_in.rearrange("b (s p) d -> p (b s) d", p=P)
            for i in range(NT // 2):
                sp.dma_start(x[:, 2 * i:2 * i + 2, :], xv[:, 2 * i:2 * i + 2, :]).then_inc(x_landed[i], 16)
                if i == 0:
                    sp.dma_start(raw[:, 4, :], lora_a.rearrange("e r d -> (e r) d")).then_inc(la_landed, 16)
                    sp.dma_start(rot[0:EXPERTS, 1, :], w_router).then_inc(la_landed, 16)
            sp.dma_start(mask[:, :], mask_in).then_inc(tables_landed, 16)
            sp.dma_start(side[:, :, :], side_in).then_inc(tables_landed, 16)
            sp.dma_start(rope[:, :, :], rope_in).then_inc(tables_landed, 16)

            def piece(slot, src):
                sp.dma_start(raw[:, slot, :] if len(src.shape) == 2 else
                             raw[:, slot, :].rearrange("p (t n) -> p t n", t=KT), src).then_inc(raw_landed[slot], 16)

            def wk_src(w, g):
                return w[:, bass.ds(g * DH, DH)].rearrange("(t p) n -> p t n", p=P)

            def wq_src(g, i):
                return wq[i * P:(i + 1) * P, bass.ds(g * (G * DH), G * DH)]

            def group(g, last):
                order = [("o", i) for i in range(G)]
                if not last:
                    order += [("k", 0)] + [("q", i) for i in range(KT)] + [("v", 0)]
                for kind, i in order:
                    if kind == "k":
                        sp.wait_ge(conv_lo, wv_lo(g))
                        off, src = 4, wk_src(wk, g + 1)
                    elif kind == "o":
                        sp.wait_ge(conv_lo, wq_lo(g, i))
                        off, src = i, wo[bass.ds(g * (G * DH) + i * DH, DH), :]
                    elif kind == "q":
                        if i < WO_POOL:
                            sp.wait_ge(conv_lo, wo_lo_pool(g, i))
                        else:
                            sp.wait_ge(wo_lo, wo_lo_dve(g, i))
                        off, src = 5 + i, wq_src(g + 1, i)
                    else:
                        sp.wait_ge(conv_lo, wk_lo(g + 1))
                        off, src = 9, wk_src(wv, g + 1)
                    piece((6 + off) % RING, src)

            sp.wait_ge(prep_tr, 6)
            piece(0, wk_src(wk, 0))
            for i in range(KT):
                piece((1 + i) % RING, wq_src(0, i))
            sp.wait_ge(conv_lo, wk_lo(0))
            piece(5 % RING, wk_src(wv, 0))
            sp.wait_ge(prep_lo, 6)
            for s in range(2):
                sp.dma_start(wb_keep[s], wb[s].bitcast(F32)).then_inc(kept, 16)
            group(0, False)
            with sp.Fori(1, KV - 1) as g:
                group(g, False)
            group(KV - 1, True)
            sp.wait_ge(kept, 32)
            sp.wait_ge(s_done, SLOTS * (2 * KV - 1))
            for s in range(2):
                sp.dma_start(wb[s].bitcast(F32), wb_keep[s]).then_inc(refetched, 16)
            ov = out.rearrange("b (s p) d -> p (b s) d", p=P)
            for t in range(NT):
                sp.wait_ge(x_out, NT + t + 1)
                sp.dma_start(ov[:, t, :], x[:, t, :]).then_inc(stored, 16)
            sp.wait_ge(stored, 16 * NT)

        @block.gpsimd
        def _(pool):
            nc.gpsimd.memset(ones, 1.0).then_inc(preset, 1)
            nc.gpsimd.memset(ebuf[:, :, :, :], -1.0).then_inc(preset, 1)
            nc.gpsimd.memset(two[:, :, :], -1.0).then_inc(preset, 1)

            def bias(f, t):
                if f == 0 and t == 0:
                    pool.wait_ge(prep_hi, 8)
                pool.wait_ge(xn_done, NT * 2 * f + t + 1)
                nc.gpsimd.tensor_tensor(x[:, t, :], x[:, t, :], half_bias[:, :], ALU.add).then_inc(biased, 1)

            steps = [0]

            def then(ins):
                steps[0] += 1
                ins.then_inc(pool_step, 1)
                pool.wait_ge(pool_step, steps[0])

            def norm_rstd(ln, t0, t1):
                pool.wait_ge(aggr, NT * ln + t1)
                rstd_steps(nc.gpsimd, then, t0, t1)
                nc.gpsimd.memset(gate_pool[:, :], 0.0).then_inc(rstd_done, 1)

            def split_lo(n, slot, hi, lo):
                pool.wait_ge(conv_hi, n + 1)
                src = raw[:, slot, :]
                if len(hi.shape) == 3:
                    src = src.rearrange("p (t n) -> p t n", t=KT)
                nc.gpsimd.tensor_tensor(lo, src, hi.bitcast(F32), ALU.subtract).then_inc(conv_lo, 1)

            def rope_sin(j, m):
                r = 5 * j + m
                w = swap[:, m % 2, :].rearrange("p (b s) -> p b s", b=2)
                tab = rope[:, 1 if m == 0 else 3, :].unsqueeze(1).broadcast_to([P, 2, SEQ])
                pool.wait_ge(swap_done, r + 1)
                nc.gpsimd.tensor_tensor(w, w, tab, ALU.mult).then_inc(t2_done, 1)

            def p_part(u, s):
                pool.wait_ge(ptlo_done, u + 1)
                both, h = pT_both[:, :, 1, s % G, :], s % G
                for blk in (2, 1):
                    last = nc.gpsimd.tensor_tensor(pT_both[:, :, blk, h, :], both.bitcast(F32),
                                                   side[:, blk - 1, :].unsqueeze(1).broadcast_to([P, 2, P]), ALU.mult)
                last.then_inc(parted, 1)

            def rope_lo(j, m, par):
                r = 5 * j + m
                hi = k[0][:, par, :] if m == 0 else q[0][:, par, m - 1, :]
                lo = k[1][:, par, :] if m == 0 else q[1][:, par, m - 1, :]
                pool.wait_ge(qhi_done, r + 1)
                nc.gpsimd.tensor_tensor(lo, rot[:, m % 2, :], hi.bitcast(F32), ALU.subtract).then_inc(qlo_done, 1)

            def weights(g, hf, s, last):
                if hf == 0 and s == 4:
                    for i in range(WO_POOL):
                        split_lo(wo_pos(g, i), (6 + i) % RING, wo_s[0][:, i, :], wo_s[1][:, i, :])
                if hf == 0 and s == 5 and not last:
                    split_lo(wk_pos(g + 1), (6 + 4) % RING, wk_s[0][:, :, :], wk_s[1][:, :, :])
                if (hf, s) in ((0, 7), (1, 0)) and not last:
                    for i in ((0, 1) if hf == 0 else (2, 3)):
                        split_lo(wq_pos(g + 1, i), (6 + 5 + i) % RING, wq_s[0][:, i, :], wq_s[1][:, i, :])
                if hf == 1 and s == 2 and not last:
                    split_lo(wv_pos(g + 1), (6 + 9) % RING, wv_s[0][:, :, :], wv_s[1][:, :, :])

            def group(g, first, last):
                for hf in range(2):
                    for s in range(SLOTS):
                        split, m = (ENDS.get(c) if not (last and hf == 1) else None for c in (s - 1, s))
                        if m is not None and m < 5:
                            rope_sin(2 * g + hf + 1, m)
                        if last and hf == 1 and s in (1, 5):
                            norm_rstd(2, s // 2, s // 2 + 2)
                        if not (first and hf == 0 and s == 0):
                            p_part(16 * g + 8 * hf + s - 1, s - 1)
                        if split is not None and split < 5:
                            rope_lo(2 * g + hf + 1, split, 1 - hf)
                        weights(g, hf, s, last)

            for t in range(NT // 2):
                bias(0, t)
            norm_rstd(0, 4, NT)
            split_lo(0, 0, wk_s[0][:, :, :], wk_s[1][:, :, :])
            for i in range(KT):
                split_lo(1 + i, (1 + i) % RING, wq_s[0][:, i, :], wq_s[1][:, i, :])
            for t in range(NT // 2, NT):
                bias(0, t)
            norm_rstd(1, 0, 2)
            norm_rstd(1, 2, 4)
            split_lo(5, 0, wv_s[0][:, :, :], wv_s[1][:, :, :])
            for m in range(6):
                if m < 5:
                    rope_sin(0, m)
                if m:
                    rope_lo(0, m - 1, 0)
            group(0, True, False)
            with pool.Fori(1, KV - 1) as g:
                group(g, False, False)
            group(KV - 1, False, True)
            p_part(16 * KV - 1, SLOTS - 1)
            for t in range(NT):
                bias(1, t)

        @block.scalar
        def _(act):
            wbv = w_base.rearrange("(c p) d -> p c d", p=P)
            for c in range(OUT // P):
                act.dma_start(raw[:, c, :], wbv[:, c, :]).then_inc(w_landed[c], 16)
            lbv = rot[:, 0, :].rearrange("p (c e r) -> p c e r", c=OUT // P, e=EXPERTS)
            for c in range(OUT // P):
                act.dma_start(lbv[:, c, :, :], lora_b[:, c * P:(c + 1) * P, :].rearrange("e p r -> p e r")).then_inc(lbr_landed, 16)
            act.dma_start(b_stage, b_base.rearrange("(a n) -> a n", a=1)).then_inc(b_landed, 16)

            def prepare_router():
                act.wait_ge(prep_tr, 1)
                nc.scalar.activation(ar[0][:, :, 0:ER], bank[2][:, :].rearrange("p (t n) -> p t n", t=KT),
                                     ACT.Copy).then_inc(prep_hi, 1)
                act.wait_ge(prep_tr, 2)
                nc.scalar.activation(ar[0][:, :, ER:ARW], bank[3][:, 0:KT * EXPERTS].rearrange("p (t n) -> p t n", t=KT),
                                     ACT.Copy).then_inc(prep_hi, 1)

            def prepare_dense(lo, hi):
                for d in range(lo, hi):
                    act.wait_ge(prep_tr, 3 + d)
                    nc.scalar.activation(wb[0][:, d, :], bank[4 + d][:, :], ACT.Copy).then_inc(prep_hi, 1)

            def prepare_lora_b():
                act.wait_ge(prep_tr, 7)
                nc.scalar.activation(lb[0][:, :], bank[6][:, :], ACT.Copy).then_inc(prep_hi, 1)
                act.wait_ge(prep_tr, 8)
                nc.scalar.activation(half_bias[:, :], bank[7][:, :], ACT.Copy, scale=0.5).then_inc(prep_hi, 1)

            def x_hi(ln, t):
                i = NT * ln + t
                act.wait_ge(tr_done, i + 1)
                nc.scalar.activation(xnT[0][:, :, t * P:(t + 1) * P],
                                     xt_bank(ln, t)[:, :].rearrange("p (c n) -> p c n", c=KT), ACT.Copy).then_inc(xhi_done, 1)

            def ht_hi(f, pr):
                p = 4 * f + pr
                act.wait_ge(ht_done, p + 1)
                wait(act, out_done, NT * f + 2 * (pr - 1))
                nc.scalar.activation(oT[0][:, pr % 2, 0, 0:2, :], ht_bank(f, pr)[:, 0:2 * P].rearrange("p (i n) -> p i n", i=2),
                                     ACT.Copy).then_inc(hthi_done, 1)

            def router_exp(f, pr):
                p = 4 * f + pr
                act.wait_ge(ar_done, p + 1)
                for i in range(2):
                    last = nc.scalar.activation(ar_part[:, i, :], S[i][:, ARW:2 * ARW], ACT.Copy)
                last.then_inc(ar_copied, 1)
                act.wait_ge(esub_done, p + 1)
                if p == 0:
                    act.wait_ge(preset, 3)
                nc.scalar.activation(ebuf[:, pr % 2, :, 0:EXPERTS], esub[:, :, :], ACT.Exp).then_inc(e_done, 1)

            def split_hi(n, slot, count, dst):
                act.wait_ge(raw_landed[slot], 16 * count)
                src = raw[:, slot, :]
                if len(dst.shape) == 3:
                    src = src.rearrange("p (t n) -> p t n", t=KT)
                nc.scalar.activation(dst, src, ACT.Copy).then_inc(conv_hi, 1)

            def weights(g, hf, s, last, part):
                def count(off):
                    return 2 * g + (6 + off) // RING + 1
                if hf == 0 and s == 4:
                    for i in part:
                        wait(act, c_done, 8 * g)
                        split_hi(wo_pos(g, i), (6 + i) % RING, count(i), wo_s[0][:, i, :])
                if hf == 0 and s == 5 and part[0] and not last:
                    act.wait_ge(a_done, 6 * (2 * g + 1) + 1)
                    split_hi(wk_pos(g + 1), (6 + 4) % RING, count(4), wk_s[0][:, :, :])
                if hf == 0 and s == 7 and not last:
                    for i in part:
                        act.wait_ge(a_done, 6 * (2 * g + 1) + 5)
                        split_hi(wq_pos(g + 1, i), (11 + i) % RING, count(5 + i), wq_s[0][:, i, :])
                if hf == 1 and s == 2 and part[0] and not last:
                    act.wait_ge(a_done, 6 * (2 * g + 1) + 6)
                    split_hi(wv_pos(g + 1), 15 % RING, count(9), wv_s[0][:, :, :])

            def rope_swap(j, m):
                r = 5 * j + m
                act.wait_ge(a_done, 6 * j + m + 1)
                wait(act, sum_done, {0: r, 1: r - 2}.get(m, r - 1))
                half = DH // 2
                for a, b in ((0, half), (half, 0)):
                    last = nc.scalar.activation(swap[a:a + half, m % 2, :], A[m % 2][b:b + half, :], ACT.Copy)
                    last.then_inc(swap_done, 1) if a else None

            def rope_hi(j, m, par):
                r = 5 * j + m
                hi = k[0][:, par, :] if m == 0 else q[0][:, par, m - 1, :]
                act.wait_ge(sum_done, r + 1)
                wait(act, s_done, SLOTS * (j - 1))
                nc.scalar.activation(hi, rot[:, m % 2, :], ACT.Copy).then_inc(qhi_done, 1)

            def v_copy(j):
                act.wait_ge(a_done, 6 * j + 6)
                act.wait_ge(sum_done, 5 * j + 4)
                nc.scalar.activation(swap[:, 1, :], A[1][:, :], ACT.Copy).then_inc(vcopy_done, 1)

            def v_hi(j, par):
                act.wait_ge(vt_done, j + 1)
                wait(act, pv_done, 4 * (j - 1))
                nc.scalar.activation(v[0][:, par, :, :], A[1][:, :].rearrange("p (t n) -> p t n", t=HT),
                                     ACT.Copy).then_inc(vhi_done, 1)

            def softmax_exp(u, s):
                act.wait_ge(min_done, u + 1)
                wait(act, t_done, u - 1)
                for i, (lo, hi) in enumerate(((0, P), (P, 2 * P))):
                    last = nc.scalar.activation(prob[:, s % 2, lo:hi], sm[:, s % 2, lo:hi], ACT.Exp,
                                                bias=nmax[:, s % 2, i:i + 1], scale=-1.0,
                                                accum_out=rsum[:, s % 2, i:i + 1])
                last.then_inc(exp_done, 1)

            def p_hi(u, s, beta):
                act.wait_ge(t_done, u + 1)
                wait(act, pv_done, 2 * beta)
                nc.scalar.activation(pT[0][:, 0:2, s % G, :], T[:, 0:2 * P].rearrange("p (c n) -> p c n", c=2),
                                     ACT.Copy).then_inc(pthi_done, 1)

            def o_hi(beta, par):
                for i in range(2):
                    act.wait_ge(pv_done, 2 * beta + i + 1)
                    wait(act, c_done, 2 * (beta - 1))
                    nc.scalar.activation(oT[0][:, par, i, :, :], O[i][:, :].rearrange("p (h n) -> p h n", h=G),
                                         ACT.Copy).then_inc(othi_done, 1)

            def group(g, first, last):
                for hf in range(2):
                    for s in range(SLOTS):
                        u, beta, b = 16 * g + 8 * hf + s, 4 * g + 2 * hf + s // G, s // G
                        start = first and hf == 0
                        softmax_exp(u, s)
                        if s == 0:
                            v_hi(2 * g + hf, hf)
                        weights(g, hf, s, last, (0, 1))
                        split, m = (ENDS.get(c) if not (last and hf == 1) else None for c in (s - 1, s))
                        if m == 5:
                            v_copy(2 * g + hf + 1)
                        elif m is not None:
                            rope_swap(2 * g + hf + 1, m)
                        if not (start and s == 0):
                            p_hi(u - 1, s - 1, beta - (s % G == 0))
                        if last and hf == 1 and s == 3:
                            x_hi(2, 0)
                            x_hi(2, 1)
                        if s % G == 1 and not (start and b == 0):
                            o_hi(beta - 1, (b + 1) % 2)
                        if split is not None and split < 5:
                            rope_hi(2 * g + hf + 1, split, 1 - hf)
                        weights(g, hf, s, last, (2, 3))

            act.wait_ge(warm_ready, 1)
            nc.scalar.activation(rsum[:, 0, 0:1], sm[:, 0, 0:1], ACT.Exp)
            prepare_router()
            prepare_dense(0, KT // 2)
            x_hi(0, 0)
            x_hi(0, 1)
            prepare_dense(KT // 2, KT)
            for pr in range(NT // 2):
                if pr == 1:
                    prepare_lora_b()
                if pr in (1, 2):
                    ht_hi(0, pr - 1)
                if pr:
                    x_hi(0, 2 * pr)
                    x_hi(0, 2 * pr + 1)
                if pr > 2:
                    ht_hi(0, pr - 1)
                router_exp(0, pr)
                if pr == 1:
                    split_hi(0, 0, 1, wk_s[0][:, :, :])
                    for i in range(KT):
                        split_hi(1 + i, (1 + i) % RING, 1, wq_s[0][:, i, :])
                if pr == 2:
                    split_hi(5, 0, 2, wv_s[0][:, :, :])
            x_hi(1, 0)
            x_hi(1, 1)
            ht_hi(0, NT // 2 - 1)
            x_hi(1, 2)
            x_hi(1, 3)
            act.wait_ge(kept, 32)
            for m in range(6):
                if m < 5:
                    rope_swap(0, m)
                if m == 4:
                    x_hi(1, 6)
                    x_hi(1, 7)
                if m:
                    rope_hi(0, m - 1, 0)
                if m == 5:
                    v_copy(0)
                if m == 3:
                    x_hi(1, 4)
                    x_hi(1, 5)
            group(0, True, False)
            with act.Fori(1, KV - 1) as g:
                group(g, False, False)
            group(KV - 1, False, True)
            p_hi(16 * KV - 1, SLOTS - 1, 4 * KV - 1)
            o_hi(4 * KV - 1, 1)
            router_exp(1, 0)
            x_hi(2, 2)
            x_hi(2, 3)
            for pr in range(1, NT // 2):
                ht_hi(1, pr - 1)
                router_exp(1, pr)
                if pr < NT // 2 - 1:
                    x_hi(2, 2 * pr + 2)
                    x_hi(2, 2 * pr + 3)
            ht_hi(1, NT // 2 - 1)

        @block.vector
        def _(dve):
            steps = [0]

            def then(ins):
                steps[0] += 1
                ins.then_inc(step, 1)
                dve.wait_ge(step, steps[0])

            def norm_stats(ln, t):
                if ln == 0 and t % 2 == 0:
                    dve.wait_ge(x_landed[t // 2], 16)
                elif ln == 1:
                    dve.wait_ge(x_out, t + 1)
                elif ln == 2:
                    dve.wait_ge(x_added, 8 * (KV - 1) + t + 1)
                then(nc.vector.bn_stats(stats[:, t, :], x[:, t, :]))
                nc.vector.bn_aggr(mv[:, t, :], stats[:, t, :]).then_inc(aggr, 1)

            def norm_rstd(ln, t0, t1):
                dve.wait_ge(aggr, NT * ln + t1)
                rstd_steps(nc.vector, then, t0, t1)

            def norm(ln, t0, t1):
                for t in range(t0, t1):
                    norm_stats(ln, t)
                norm_rstd(ln, t0, t1)

            def xn(ln, t):
                i = NT * ln + t
                wait(dve, tr_done, i - 1)
                nc.vector.tensor_scalar(xn_buf(ln, t), x[:, t, :].rearrange("p (a n) -> p a n", a=2), mv[:, t, 0:1], rstd[:, t:t + 1],
                                        ALU.subtract, ALU.mult).then_inc(xn_done, 1)

            def x_lo(ln, t):
                i = NT * ln + t
                dve.wait_ge(xhi_done, i + 1)
                c = slice(t * P, (t + 1) * P)
                nc.vector.tensor_tensor(xnT[1][:, :, c], xt_bank(ln, t)[:, :].rearrange("p (c n) -> p c n", c=KT),
                                        xnT[0][:, :, c].bitcast(F32), ALU.subtract).then_inc(xlo_done, 1)

            def router(f, pr):
                p = 4 * f + pr
                eb = ebuf[:, pr % 2, :, :]
                dve.wait_ge(ar_copied, p + 1)
                for i in range(2):
                    last = nc.vector.tensor_tensor(logits[:, i, :], S[i][:, ER:ARW], ar_part[:, i, ER:ARW], ALU.add)
                then(last)
                for i in range(2):
                    last = nc.vector.max(top[:, i, :], logits[:, i, :])
                then(last)
                nc.vector.tensor_tensor(esub[:, :, :], logits[:, :, :], top[:, :, 0:1].broadcast_to([P, 2, EXPERTS]),
                                        ALU.subtract).then_inc(esub_done, 1)
                wait(dve, ht_done, p)
                for i in range(2):
                    nc.vector.tensor_tensor(sm[:, i, 0:ER], S[i][:, 0:ER], ar_part[:, i, 0:ER], ALU.add)
                dve.wait_ge(e_done, p + 1)
                if p == 0:
                    dve.wait_ge(preset, 3)
                for i in range(2):
                    last = nc.vector.max(etop[:, i, :], eb[:, i, 0:EXPERTS])
                then(last)
                nc.vector.tensor_tensor(esum[:, :], etop[:, :, 0], etop[:, :, 1], ALU.add)
                then(nc.vector.tensor_copy(two[:, :, 0:2], etop[:, :, 0:2]))
                for i in range(2):
                    last = nc.vector.match_replace(rest[:, i, :], two[:, i, :], eb[:, i, :], 0.0)
                then(last)
                nc.vector.reciprocal(einv[:, :], esum[:, :])
                then(nc.vector.tensor_tensor(wgt[:, :, :], eb[:, :, 0:EXPERTS], rest[:, :, 0:EXPERTS], ALU.subtract))
                then(nc.vector.tensor_tensor(wgt[:, :, :], wgt[:, :, :],
                                             einv[:, :].unsqueeze(2).broadcast_to([P, 2, EXPERTS]), ALU.mult))
                for i in range(2):
                    h = sm[:, i, 0:ER].rearrange("p (e r) -> p e r", e=EXPERTS)
                    last = nc.vector.scalar_tensor_tensor(
                        h, h, 2.0,
                        wgt[:, i, :].unsqueeze(2).broadcast_to([P, EXPERTS, RANK]), ALU.mult, ALU.mult)
                last.then_inc(hw_done, 1)

            def ht_lo(f, pr):
                p = 4 * f + pr
                dve.wait_ge(hthi_done, p + 1)
                nc.vector.tensor_tensor(oT[1][:, pr % 2, 0, 0:2, :], ht_bank(f, pr)[:, 0:2 * P].rearrange("p (i n) -> p i n", i=2),
                                        oT[0][:, pr % 2, 0, 0:2, :].bitcast(F32), ALU.subtract).then_inc(htlo_done, 1)

            def ffn_out(f, pr):
                for i in range(2):
                    t = 2 * pr + i
                    dve.wait_ge(out_done, NT * f + t + 1)
                    dve.wait_ge(biased, NT * f + t + 1)
                    nc.vector.scalar_tensor_tensor(x[:, t, :], OUTB[f][pr % 2][i][:, :], 0.5, x[:, t, :],
                                                   ALU.mult, ALU.add).then_inc(x_out, 1)

            def prepare_router():
                dve.wait_ge(prep_hi, 1)
                nc.vector.tensor_tensor(ar[1][:, :, 0:ER], bank[2][:, :].rearrange("p (t n) -> p t n", t=KT),
                                        ar[0][:, :, 0:ER].bitcast(F32), ALU.subtract).then_inc(prep_lo, 1)
                dve.wait_ge(prep_hi, 2)
                nc.vector.tensor_tensor(ar[1][:, :, ER:ARW], bank[3][:, 0:KT * EXPERTS].rearrange("p (t n) -> p t n", t=KT),
                                        ar[0][:, :, ER:ARW].bitcast(F32), ALU.subtract).then_inc(prep_lo, 1)

            def prepare_dense():
                for d in range(KT):
                    dve.wait_ge(prep_hi, 3 + d)
                    nc.vector.tensor_tensor(wb[1][:, d, :], bank[4 + d][:, :], wb[0][:, d, :].bitcast(F32),
                                            ALU.subtract).then_inc(prep_lo, 1)

            def prepare_lora_b():
                dve.wait_ge(prep_hi, 7)
                nc.vector.tensor_tensor(lb[1][:, :], bank[6][:, :], lb[0][:, :].bitcast(F32),
                                        ALU.subtract).then_inc(prep_lo, 1)

            def rope_cos(j, m):
                r = 5 * j + m
                dve.wait_ge(swap_done, r + 1)
                wait(dve, qlo_done, {0: r, 1: r - 2}.get(m, r - 1))
                nc.vector.tensor_tensor(rot[:, m % 2, :].rearrange("p (b s) -> p b s", b=2),
                                        A[m % 2][:, :].rearrange("p (b s) -> p b s", b=2),
                                        rope[:, 0 if m == 0 else 2, :].unsqueeze(1).broadcast_to([P, 2, SEQ]),
                                        ALU.mult).then_inc(a_free, 1)

            def rope_sum(j, m):
                r = 5 * j + m
                dve.wait_ge(t2_done, r + 1)
                dve.wait_ge(a_free, 6 * j + m + 1)
                nc.vector.tensor_tensor(rot[:, m % 2, :], rot[:, m % 2, :], swap[:, m % 2, :],
                                        ALU.add).then_inc(sum_done, 1)

            def v_lo(j, par):
                dve.wait_ge(vhi_done, j + 1)
                nc.vector.tensor_tensor(v[1][:, par, :, :], A[1][:, :].rearrange("p (t n) -> p t n", t=HT),
                                        v[0][:, par, :, :].bitcast(F32), ALU.subtract).then_inc(a_free, 1)

            def softmax_min(u, s):
                dve.wait_ge(s_done, u + 1)
                wait(dve, exp_done, u - 1)
                sc = S[s % 2]
                nc.vector.tensor_tensor(sm[:, s % 2, 0:P], sc[:, P:2 * P], mask[:, 0:P], ALU.add).then_inc(part_done, 1)
                nc.vector.tensor_tensor_reduce(sm[:, s % 2, P:3 * P], sc[:, 2 * P:4 * P], mask[:, P:3 * P],
                                               1.0, FMAX, ALU.add, ALU.min, nmax[:, s % 2, 1:2]).then_inc(part_done, 1)
                dve.wait_ge(part_done, 2 * u + 2)
                nc.vector.memset(gate[:, :], 0.0)
                nc.vector.tensor_tensor_reduce(sm[:, s % 2, 0:P], sc[:, 0:P], sm[:, s % 2, 0:P], 1.0, FMAX,
                                               ALU.add, ALU.min, nmax[:, s % 2, 0:1])
                nc.vector.tensor_tensor(sm[:, s % 2, P:2 * P], sm[:, s % 2, P:2 * P], sm[:, s % 2, 2 * P:3 * P],
                                        ALU.min).then_inc(min_done, 1)

            def softmax_norm(u, s):
                dve.wait_ge(exp_done, u + 1)
                nc.vector.reciprocal(rinv[:, s % 2, :], rsum[:, s % 2, :]).then_inc(rinv_done, 1)
                dve.wait_ge(rinv_done, u + 1)
                for i, (lo, hi) in enumerate(((0, P), (P, 2 * P))):
                    last = nc.vector.tensor_scalar(prob[:, s % 2, lo:hi], prob[:, s % 2, lo:hi],
                                                   rinv[:, s % 2, i:i + 1], None, ALU.mult)
                last.then_inc(norm_done, 1)

            def p_lo(u, s):
                dve.wait_ge(pthi_done, u + 1)
                nc.vector.tensor_tensor(pT[1][:, 0:2, s % G, :], T[:, 0:2 * P].rearrange("p (c n) -> p c n", c=2),
                                        pT[0][:, 0:2, s % G, :].bitcast(F32), ALU.subtract).then_inc(ptlo_done, 1)

            def o_lo(beta, par):
                for i in range(2):
                    dve.wait_ge(othi_done, 2 * beta + i + 1)
                    nc.vector.tensor_tensor(oT[1][:, par, i, :, :], O[i][:, :].rearrange("p (h n) -> p h n", h=G),
                                            oT[0][:, par, i, :, :].bitcast(F32), ALU.subtract).then_inc(otlo_done, 1)

            def x_add(beta, b, i):
                dve.wait_ge(c_done, 2 * beta + i + 1)
                wait(dve, x_added, 2 * beta + i)
                nc.vector.tensor_tensor(x[:, 2 * b + i, :], C[:, :], x[:, 2 * b + i, :], ALU.add).then_inc(x_added, 1)

            def ffn_start(s):
                if s in (0, 4):
                    norm_stats(2, s // 2)
                    norm_stats(2, s // 2 + 1)
                if s == 2:
                    dve.wait_ge(sum_done, 5 * 2 * KV)
                    dve.wait_ge(vt_done, 2 * KV)
                if s in (2, 7):
                    dve.wait_ge(rstd_done, 5 if s == 7 else 4)
                    xn(2, 2 if s == 7 else 0)
                    xn(2, 3 if s == 7 else 1)
                if s == 3:
                    x_lo(2, 0)
                    x_lo(2, 1)

            def wo_split(g):
                for i in range(WO_POOL, G):
                    dve.wait_ge(conv_hi, wo_pos(g, i) + 1)
                    nc.vector.tensor_tensor(wo_s[1][:, i, :], raw[:, (6 + i) % RING, :], wo_s[0][:, i, :].bitcast(F32),
                                            ALU.subtract).then_inc(wo_lo, 1)

            def group(g, first, last):
                for hf in range(2):
                    for s in range(SLOTS):
                        u, beta, b = 16 * g + 8 * hf + s, 4 * g + 2 * hf + s // G, 2 * hf + s // G
                        start = first and b == 0
                        split, m = (ENDS.get(c) if not (last and hf == 1) else None for c in (s - 1, s))
                        if s == 0 and not (last and hf == 1):
                            v_lo(2 * g + hf, hf)
                        if s % G == 3 and not start:
                            x_add(beta - 1, (b - 1) % BATCH, 0)
                        if s % G == 0 and not (first and b < 2):
                            x_add(beta - 2, (b - 2) % BATCH, 1)
                        softmax_norm(u, s)
                        if hf == 0 and s == 5:
                            wo_split(g)
                        if split is not None and split < 5:
                            rope_sum(2 * g + hf + 1, split)
                        if m is not None and m < 5:
                            rope_cos(2 * g + hf + 1, m)
                        if not (start and s == 0):
                            p_lo(u - 1, s - 1)
                        if s == 0 and last and hf == 1:
                            v_lo(2 * g + hf, hf)
                        if not (last and hf == 1 and s == SLOTS - 1):
                            softmax_min(u + 1, (s + 1) % SLOTS)
                        if s % G == 1 and not start:
                            o_lo(beta - 1, (b + 1) % 2)
                        if last and hf == 1:
                            ffn_start(s)

            nc.vector.memset(sm[:, 0, :], 0.0).then_inc(warm_ready, 1)
            norm(0, 0, 2)
            xn(0, 0)
            xn(0, 1)
            prepare_router()
            norm_stats(0, 2)
            norm_stats(0, 3)
            x_lo(0, 0)
            x_lo(0, 1)
            prepare_dense()
            router(0, 0)
            norm_rstd(0, 2, 4)
            xn(0, 2)
            xn(0, 3)
            prepare_lora_b()
            ht_lo(0, 0)
            x_lo(0, 2)
            x_lo(0, 3)
            for t in range(4, NT):
                norm_stats(0, t)
            for pr in range(1, NT // 2):
                ln, t = (0, 2 * pr + 2) if pr < NT // 2 - 1 else (1, 0)
                if pr == 1:
                    router(0, pr)
                if pr != 2:
                    dve.wait_ge(rstd_done, 1 + pr // 2)
                    xn(ln, t)
                    xn(ln, t + 1)
                if pr > 1:
                    router(0, pr)
                else:
                    ht_lo(0, pr)
                x_lo(ln, t)
                x_lo(ln, t + 1)
                if pr == 1:
                    xn(0, 6)
                    xn(0, 7)
                if ln == 1:
                    dve.wait_ge(rstd_done, 3)
                    xn(1, 2)
                    xn(1, 3)
                if ln == 1:
                    ht_lo(0, pr)
                    x_lo(1, 2)
                    x_lo(1, 3)
                ffn_out(0, pr - 1)
                norm_stats(1, 2 * pr - 2)
                if pr == 2:
                    ht_lo(0, pr)
                norm_stats(1, 2 * pr - 1)
            ffn_out(0, NT // 2 - 1)
            dve.wait_ge(tables_landed, 48)
            rope_cos(0, 0)
            norm_stats(1, NT - 2)
            rope_sum(0, 0)
            rope_cos(0, 1)
            norm_stats(1, NT - 1)
            rope_sum(0, 1)
            rope_cos(0, 2)
            norm_rstd(1, 4, NT)
            xn(1, 4)
            xn(1, 5)
            rope_sum(0, 2)
            rope_cos(0, 3)
            xn(1, 6)
            xn(1, 7)
            x_lo(1, 4)
            x_lo(1, 5)
            rope_sum(0, 3)
            rope_cos(0, 4)
            x_lo(1, 6)
            x_lo(1, 7)
            rope_sum(0, 4)
            softmax_min(0, 0)
            group(0, True, False)
            with dve.Fori(1, KV - 1) as g:
                group(g, False, False)
            group(KV - 1, False, True)
            x_add(4 * KV - 2, BATCH - 2, 1)
            p_lo(16 * KV - 1, SLOTS - 1)
            o_lo(4 * KV - 1, 1)
            router(1, 0)
            x_add(4 * KV - 1, BATCH - 1, 0)
            norm_stats(2, 4)
            norm_stats(2, 5)
            x_lo(2, 2)
            x_lo(2, 3)
            ht_lo(1, 0)
            x_add(4 * KV - 1, BATCH - 1, 1)
            norm_stats(2, 6)
            norm_stats(2, 7)
            norm_rstd(2, 4, NT)
            for pr in range(1, NT // 2):
                if pr > 1:
                    ht_lo(1, pr - 1)
                if pr < NT // 2 - 1:
                    xn(2, 2 * pr + 2)
                    xn(2, 2 * pr + 3)
                router(1, pr)
                if pr < NT // 2 - 1:
                    x_lo(2, 2 * pr + 2)
                    x_lo(2, 2 * pr + 3)
                ffn_out(1, pr - 1)
            ht_lo(1, NT // 2 - 1)
            ffn_out(1, NT // 2 - 1)

        @block.tensor
        def _(pe):
            mm, tp = nc.tensor.matmul, nc.tensor.transpose

            def prepare():
                pe.wait_ge(warm_ready, 1)
                for _ in range(WARM):
                    mm(bank[7][:, 0:3 * P], sm[:, 0, 0:P], sm[:, 0, :], start=True, stop=True)
                pe.wait_ge(ident_landed, 16)
                pe.wait_ge(la_landed, 32)
                for d in range(KT):
                    last = tp(bank[2][:, d * P:(d + 1) * P], raw[:, 4, d * P:(d + 1) * P], ident[:, :])
                last.then_inc(prep_tr, 1)
                for d in range(KT):
                    last = tp(bank[3][:, d * EXPERTS:(d + 1) * EXPERTS], rot[0:EXPERTS, 1, d * P:(d + 1) * P],
                              ident[0:EXPERTS, 0:EXPERTS])
                last.then_inc(prep_tr, 1)
                for c in range(OUT // P):
                    pe.wait_ge(w_landed[c], 16)
                    for d in range(KT):
                        last = tp(bank[4 + d][:, c * P:(c + 1) * P], raw[:, c, d * P:(d + 1) * P], ident[:, :])
                        if c == OUT // P - 1:
                            last.then_inc(prep_tr, 1)

            def prepare_lora_b():
                pe.wait_ge(lbr_landed, 16 * (OUT // P))
                for c in range(OUT // P):
                    last = tp(bank[6][:, c * P:(c + 1) * P], rot[:, 0, c * P:(c + 1) * P], ident[:, :])
                last.then_inc(prep_tr, 1)
                pe.wait_ge(b_landed, 16)
                pe.wait_ge(preset, 1)
                mm(bank[7][:, :], ones, b_stage, start=True, stop=True).then_inc(prep_tr, 1)

            def x_transpose(ln, t):
                i = NT * ln + t
                pe.wait_ge(xn_done, i + 1)
                wait(pe, xlo_done, i - 1)
                for c in range(KT):
                    last = tp(xt_bank(ln, t)[:, c * P:(c + 1) * P], xn_buf(ln, t)[:, c // 2, c % 2 * P:(c % 2 + 1) * P], ident[:, :])
                last.then_inc(tr_done, 1)

            def lora_router(f, pr):
                for i in range(2):
                    c = slice((2 * pr + i) * P, (2 * pr + i + 1) * P)
                    pe.wait_ge(xhi_done, NT * 2 * f + 2 * pr + i + 1)
                    if f == 1 and pr == 0:
                        pe.wait_ge(min_done, 16 * KV - 1 + i)
                    for d in range(KT):
                        mm(S[i][:, 0:2 * ARW], xnT[0][:, d, c], ar_both[:, d, :, :], start=(d == 0), stop=False)
                for i in range(2):
                    c = slice((2 * pr + i) * P, (2 * pr + i + 1) * P)
                    pe.wait_ge(xlo_done, NT * 2 * f + 2 * pr + i + 1)
                    for d in range(KT):
                        last = mm(S[i][:, 0:ARW], xnT[1][:, d, c], ar[0][:, d, :], start=False, stop=(d == KT - 1))
                last.then_inc(ar_done, 1)

            def dense(f, pr, lo=0, hi=24):
                for step_ in range(lo, hi):
                    i, n, d = step_ // 12, step_ % 12 // KT, step_ % KT
                    if step_ == 0 and pr >= 2:
                        pe.wait_ge(x_out, NT * f + 2 * pr - 2)
                    a, b = PASSES[n]
                    mm(OUTB[f][pr % 2][i][:, :], xnT[a][:, d, (2 * pr + i) * P:(2 * pr + i + 1) * P], wb[b][:, d, :],
                       start=(n == 0 and d == 0), stop=False)

            def h_transpose(f, pr):
                p = 4 * f + pr
                pe.wait_ge(hw_done, p + 1)
                if ht_bank(f, pr) in (bank[0], bank[4]):
                    pe.wait_ge(xlo_done, NT * 2 * f + min(2 * pr + 3, NT))
                for i in range(2):
                    last = tp(ht_bank(f, pr)[:, i * P:(i + 1) * P], sm[:, i, 0:ER], ident[:, :])
                last.then_inc(ht_done, 1)

            def lora_out(f, pr):
                pe.wait_ge(htlo_done, 4 * f + pr + 1)
                for i in range(2):
                    for n, (a, b) in enumerate(PASSES):
                        last = mm(OUTB[f][pr % 2][i][:, :], oT[a][:, pr % 2, 0, i, :], lb[b][:, :],
                                  start=False, stop=(n == 2))
                    last.then_inc(out_done, 1)

            def project(j, hf, lo, hi, g):
                for n in range(lo, hi):
                    m, i = n // 12, n % 12
                    if i == 0:
                        wait(pe, a_free, 6 * j + m - 1)
                    if hf == 0 and i == 0 and m in (0, 1, 5):
                        pe.wait_ge(conv_hi, {0: wk_pos(g), 1: wq_pos(g, KT - 1), 5: wv_pos(g)}[m] + 1)
                    if hf == 0 and i == 2 * KT and m in (0, 1, 5):
                        pe.wait_ge(conv_lo, {0: wk_lo(g), 1: wq_lo(g, KT - 1), 5: wv_lo(g)}[m])
                    a, b = PASSES[i // KT]
                    d = i % KT
                    w = wk_s[a][:, d, :] if m == 0 else wv_s[a][:, d, :] if m == 5 else wq_s[a][:, d, (m - 1) * DH:m * DH]
                    last = mm(A[m % 2][:, :], w, xnT[b][:, d, hf * HALF:(hf + 1) * HALF],
                              start=(i == 0), stop=(i == 11))
                    if i == 11:
                        last.then_inc(a_done, 1)

            def v_transpose(j):
                pe.wait_ge(vcopy_done, j + 1)
                for t in range(HT):
                    last = tp(A[1][:, t * DH:(t + 1) * DH], swap[:, 1, t * P:(t + 1) * P], ident[:, :])
                last.then_inc(vt_done, 1)

            def scores(u, s, j, hf):
                b, h = s // G, s % G
                pe.wait_ge(qlo_done, 5 * j + 2 + h)
                wait(pe, min_done, u - 1)
                q0, q1 = (slice(b * SEQ + i * P, b * SEQ + (i + 1) * P) for i in range(2))
                mm(S[s % 2][:, 0:2 * P], q[0][:, hf, h, q0], k_both[:, :, hf, q0], start=True, stop=False)
                mm(S[s % 2][:, 0:P], q[1][:, hf, h, q0], k[0][:, hf, q0], start=False, stop=True)
                for n, (a, c) in enumerate(PASSES):
                    last = mm(S[s % 2][:, 2 * P:4 * P], q[a][:, hf, h, q1], k[c][:, hf, b * SEQ:(b + 1) * SEQ],
                              start=(n == 0), stop=(n == 2))
                last.then_inc(s_done, 1)

            def p_transpose(u, s):
                pe.wait_ge(norm_done, u + 1)
                wait(pe, ptlo_done, u)
                for c in range(2):
                    last = tp(T[:, c * P:(c + 1) * P], prob[:, s % 2, c * P:(c + 1) * P], ident[:, :])
                last.then_inc(t_done, 1)

            def values(beta, par, b, j):
                pe.wait_ge(a_free, 6 * j + 6)
                pe.wait_ge(ptlo_done, 4 * beta + 4)
                wait(pe, otlo_done, 2 * beta)
                for i, blocks in enumerate((((0, 0),), ((1, 0), (2, 1)))):
                    if i:
                        pe.wait_ge(parted, 4 * beta + 4)
                    todo = [(blk, kb, a, c) for blk, kb in blocks for a, c in PASSES]
                    for n, (blk, kb, a, c) in enumerate(todo):
                        last = mm(O[i][:, :], v[a][:, par, 2 * b + kb, :], pT[c][:, blk, :, :],
                                  start=(n == 0), stop=(n == len(todo) - 1))
                    last.then_inc(pv_done, 1)

            def out_project(beta, par, i, g):
                pe.wait_ge(conv_hi, wo_pos(g, G - 1) + 1)
                pe.wait_ge(othi_done, 2 * beta + i + 1)
                wait(pe, x_added, 2 * beta + i)
                for n, (a, c) in enumerate(((0, 0), (0, 1), (1, 0))):
                    if c:
                        pe.wait_ge(conv_lo, wo_lo_pool(g, WO_POOL - 1))
                        pe.wait_ge(wo_lo, wo_lo_dve(g, G - 1))
                    if a:
                        pe.wait_ge(otlo_done, 2 * beta + i + 1)
                    for h in range(G):
                        last = mm(C[:, :], oT[a][:, par, i, h, :], wo_s[c][:, h, :],
                                  start=(h == 0 and n == 0), stop=(h == G - 1 and n == 2))
                last.then_inc(c_done, 1)

            def group(g, first, last):
                for hf in range(2):
                    j = 2 * g + hf
                    for s in range(SLOTS):
                        u, beta, b = 16 * g + 8 * hf + s, 4 * g + 2 * hf + s // G, 2 * hf + s // G
                        start = first and b == 0
                        if s == 0 and not start:
                            v_transpose(j)
                        if start and s == 0:
                            pe.wait_ge(xlo_done, 2 * NT)
                        if not (last and hf == 1):
                            project(j + 1, 1 - hf, FIRST[s], FIRST[s + 1], g + hf)
                        elif s >= 4:
                            if s == 4:
                                pe.wait_ge(refetched, 32)
                                pe.wait_ge(xlo_done, 2 * NT + 2)
                            dense(1, 0, 6 * (s - 4), 6 * (s - 3))
                        if s == 0 and start:
                            v_transpose(j)
                        prev_hf = ((b - 1) % BATCH) // 2
                        if s < SLOTS - 1:
                            scores(u + 1, s + 1, j, hf)
                        elif not (last and hf == 1):
                            scores(u + 1, 0, j + 1, 1 - hf)
                        if not (start and s == 0):
                            p_transpose(u - 1, s - 1)
                        if last and hf == 1 and s == 3:
                            x_transpose(2, 0)
                            x_transpose(2, 1)
                        if s % G == 1 and not start:
                            values(beta - 1, prev_hf, (b - 1) % 2, j - (s < G))
                        if s % G >= 2 and not start:
                            out_project(beta - 1, (b - 1) % 2, s % G - 2, g if b else g - 1)

            prepare()
            x_transpose(0, 0)
            x_transpose(0, 1)
            pe.wait_ge(prep_lo, 2)
            lora_router(0, 0)
            pe.wait_ge(prep_lo, 4)
            pe.wait_ge(prep_hi, 6)
            dense(0, 0, 0, KT)
            pe.wait_ge(prep_lo, 6)
            dense(0, 0, KT, 24)
            prepare_lora_b()
            h_transpose(0, 0)
            x_transpose(0, 2)
            x_transpose(0, 3)
            pe.wait_ge(prep_lo, 7)
            pe.wait_ge(prep_hi, 8)
            lora_out(0, 0)
            for pr in range(1, NT // 2):
                lora_router(0, pr)
                before = 8 if pr == NT // 2 - 1 else 0
                if pr > 2:
                    dense(0, pr, 0, before)
                    lora_out(0, pr - 1)
                ln, t = (0, 2 * pr + 2) if pr < NT // 2 - 1 else (1, 0)
                if pr == 1:
                    dense(0, pr)
                    h_transpose(0, pr)
                x_transpose(ln, t)
                x_transpose(ln, t + 1)
                if pr > 1:
                    dense(0, pr, before, 24)
                    h_transpose(0, pr)
                else:
                    lora_out(0, pr)
            x_transpose(1, 2)
            x_transpose(1, 3)
            lora_out(0, NT // 2 - 1)
            pe.wait_ge(xlo_done, NT + NT // 2)
            for m in range(5):
                project(0, 0, 12 * m, 12 * (m + 1), 0)
            x_transpose(1, 4)
            x_transpose(1, 5)
            project(0, 0, 60, 60 + 8, 0)
            pe.wait_ge(x_out, 6)
            x_transpose(1, 6)
            x_transpose(1, 7)
            project(0, 0, 60 + 8, 72, 0)
            scores(0, 0, 0, 0)
            group(0, True, False)
            with pe.Fori(1, KV - 1) as g:
                group(g, False, False)
            group(KV - 1, False, True)
            p_transpose(16 * KV - 1, SLOTS - 1)
            lora_router(1, 0)
            values(4 * KV - 1, 1, 1, 2 * KV - 1)
            out_project(4 * KV - 1, 1, 0, KV - 1)
            pe.wait_ge(ptlo_done, 16 * KV)
            x_transpose(2, 2)
            x_transpose(2, 3)
            h_transpose(1, 0)
            out_project(4 * KV - 1, 1, 1, KV - 1)
            lora_out(1, 0)
            for pr in range(1, NT // 2):
                lora_router(1, pr)
                if pr > 1:
                    lora_out(1, pr - 1)
                before = 16 if pr == 1 else 0
                if pr == 1:
                    pe.wait_ge(x_added, 8 * KV)
                dense(1, pr, 0, before)
                if pr < NT // 2 - 1:
                    x_transpose(2, 2 * pr + 2)
                    x_transpose(2, 2 * pr + 3)
                dense(1, pr, before, 16 if pr == NT // 2 - 1 else 24)
                h_transpose(1, pr)
                if pr == NT // 2 - 1:
                    dense(1, pr, 16, 24)
            lora_out(1, NT // 2 - 1)


_INS = ["L0_attn_x", "L0_attn_wq", "L0_attn_wk", "L0_attn_wv", "L0_attn_wo", "L0_ffn_W_base", "L0_ffn_b_base",
        "L0_ffn_W_router", "L0_ffn_lora_A", "L0_ffn_lora_B"]


def kernel(**inputs):
    import concourse.bacc as bacc
    from concourse.bass_utils import run_bass_kernel_spmd

    nc = bacc.Bacc("TRN2", target_bir_lowering=False, num_devices=1)
    arrays, args = {}, []
    for name in _INS:
        arrays[f"in_{name}"] = np.ascontiguousarray(inputs[name])
    for name, a in zip(("ident", "mask", "side", "rope"), constants()):
        arrays[f"const_{name}"] = a
    for name, a in arrays.items():
        args.append(nc.dram_tensor(name, a.shape, mybir.dt.from_np(a.dtype), kind="ExternalInput").ap())
    args.append(nc.dram_tensor("out", (BATCH, SEQ, HID), F32, kind="ExternalOutput").ap())
    macaron(nc, *args)
    r = run_bass_kernel_spmd(nc, [arrays], core_ids=[0])
    return r.results[0]["out"]
```
